# Optimizing a Trainium2 kernel written in Bass

```python
import numpy as np
import jax
import jax.numpy as jnp

def _softmax(x, axis=-1):
    return jax.nn.softmax(x, axis=axis)

def _gelu(x):
    return jax.nn.gelu(x, approximate=True)

def _silu(x):
    return jax.nn.silu(x)

def _sigmoid(x):
    return jax.nn.sigmoid(x)

def _layernorm(x, axis=-1, eps=1e-05):
    m = jnp.mean(x, axis=axis, keepdims=True)
    v = jnp.var(x, axis=axis, keepdims=True)
    return (x - m) / jnp.sqrt(v + eps)

def _scatter_add(tgt, idx, src, axis=0):
    return tgt.at[idx].add(src)

def _segment_sum(src, seg, n):
    return jax.ops.segment_sum(src, seg, n)
kernel_name = 'mk_adaln_d2_jaxref_r8_752cd1'

def setup_inputs(seed: int=0):
    np.random.seed(seed)
    _w = jnp.asarray

    def _L0_attn_setup():
        import jax, jax.numpy as jnp
        import numpy as np
        B, S, HID = (2, 256, 256)
        H, D, K = (16, 128, 4)
        ROPE_BASE = 1000000.0
        EPS_NORM = 1e-06

        def _silu(u):
            return u * jax.nn.sigmoid(u)

        def _causal_dwconv(x_bsc, w_ck):
            C, Kw = w_ck.shape
            y = jax.lax.conv_general_dilated(x_bsc.transpose(0, 2, 1), w_ck[:, None, :], (1,), [(Kw - 1, 0)], dimension_numbers=('NCH', 'OIH', 'NCH'), feature_group_count=C)
            return y.transpose(0, 2, 1)

        def _lag(u, s):
            if s == 0:
                return u
            pad = [(0, 0), (s, 0)] + [(0, 0)] * (u.ndim - 2)
            return jnp.pad(u, pad)[:, :u.shape[1]]
        key = jax.random.key(seed)
        ks = jax.random.split(key, 12)
        p = lambda k, shape: jax.random.normal(k, shape, jnp.float32) * 0.02
        x = jax.random.normal(ks[0], (B, S, HID), jnp.float32)
        return {'x': x, 'Wq': p(ks[1], (HID, H * D)), 'Wk': p(ks[2], (HID, H * D)), 'Wv': p(ks[3], (HID, H * D)), 'Wz': p(ks[4], (HID, H * D)), 'Wa': p(ks[5], (HID, H)), 'Wb': p(ks[6], (HID, H)), 'conv_q_w': p(ks[7], (H * D, K)), 'conv_k_w': p(ks[8], (H * D, K)), 'conv_v_w': p(ks[9], (H * D, K)), 'norm_w': jnp.ones((H * D,), jnp.float32), 'Wout': p(ks[10], (H * D, HID))}
    _L0_attn_in = _L0_attn_setup()

    def _L0_ffn_setup():
        import jax, jax.numpy as jnp
        import numpy as np
        HIDDEN = 256
        INTER = 688
        LUT_SIZE = 16

        def _ghost_linear(x, idx, lut):
            w = lut[idx]
            return jnp.einsum('bsh,oh->bso', x, w)
        key = jax.random.key(seed)
        k_x, k_lut, k_g, k_u, k_d = jax.random.split(key, 5)
        x = jax.random.normal(k_x, (2, 512, HIDDEN), dtype=jnp.float32)
        lut = jax.random.normal(k_lut, (LUT_SIZE,), dtype=jnp.float32) * 0.02
        gate_idx = jax.random.randint(k_g, (INTER, HIDDEN), 0, LUT_SIZE, dtype=jnp.int32)
        up_idx = jax.random.randint(k_u, (INTER, HIDDEN), 0, LUT_SIZE, dtype=jnp.int32)
        down_idx = jax.random.randint(k_d, (HIDDEN, INTER), 0, LUT_SIZE, dtype=jnp.int32)
        return {'x': x, 'lut': lut, 'gate_idx': gate_idx, 'up_idx': up_idx, 'down_idx': down_idx}
    _L0_ffn_in = _L0_ffn_setup()
    _L0_c = _w((lambda *s: np.random.randn(*s).astype(np.float32) * 0.05)(4, 256))
    _L0_wmod = _w((lambda *s: np.random.randn(*s).astype(np.float32) * 0.05)(256, 6 * 256) * 256 ** (-0.5))

    def _L1_attn_setup():
        import jax, jax.numpy as jnp
        import numpy as np
        BLOCK = 32
        NUM_HEADS = 16
        HEAD_DIM = 128
        FP4_GRID = jnp.array([0.0, 0.5, 1.0, 1.5, 2.0, 3.0, 4.0, 6.0], dtype=jnp.float32)

        def quantize_to_mxfp4(w, block_size=BLOCK):
            D, F = w.shape
            blocks = w.reshape(D // block_size, block_size, F)
            amax = jnp.max(jnp.abs(blocks), axis=1)
            e = jnp.floor(jnp.log2(jnp.maximum(amax, 1e-12) / 6.0))
            scale = jnp.exp2(e)
            v = blocks / scale[:, None, :]
            idx = jnp.argmin(jnp.abs(jnp.abs(v)[..., None] - FP4_GRID), axis=-1)
            codes = jnp.sign(v) * FP4_GRID[idx]
            return (codes.reshape(D, F).astype(jnp.float32), scale.astype(jnp.float32))

        def _mxfp4_matmul(x, codes, scales, block_size=BLOCK):
            w = codes * jnp.repeat(scales, block_size, axis=0)
            return x @ w
        key = jax.random.key(seed)
        ks = jax.random.split(key, 9)
        B, S, D = (2, 256, 256)
        feat = NUM_HEADS * HEAD_DIM
        x = jax.random.normal(ks[0], (B, S, D), dtype=jnp.float32)

        def make_w(k, din, dout):
            w = jax.random.normal(k, (din, dout), dtype=jnp.float32) * (1.0 / np.sqrt(din))
            return quantize_to_mxfp4(w, BLOCK)
        wq_codes, wq_scales = make_w(ks[1], D, feat)
        wk_codes, wk_scales = make_w(ks[2], D, feat)
        wv_codes, wv_scales = make_w(ks[3], D, feat)
        wo_codes, wo_scales = make_w(ks[4], feat, D)
        bq = jnp.zeros((feat,), jnp.float32)
        bk = jnp.zeros((feat,), jnp.float32)
        bv = jnp.zeros((feat,), jnp.float32)
        bo = jnp.zeros((D,), jnp.float32)
        return {'x': x, 'wq_codes': wq_codes, 'wq_scales': wq_scales, 'bq': bq, 'wk_codes': wk_codes, 'wk_scales': wk_scales, 'bk': bk, 'wv_codes': wv_codes, 'wv_scales': wv_scales, 'bv': bv, 'wo_codes': wo_codes, 'wo_scales': wo_scales, 'bo': bo}
    _L1_attn_in = _L1_attn_setup()

    def _L1_ffn_setup():
        import jax, jax.numpy as jnp
        import numpy as np
        H = 256
        I = 128
        E = 32
        K = 4
        N_SHARED = 1
        EPS = 1e-06

        def _rmsnorm(x, w, eps=EPS):
            var = jnp.mean(jnp.square(x), axis=-1, keepdims=True)
            return x * jax.lax.rsqrt(var + eps) * w

        def _moe_core(x, gate_w, w13, w2):
            T = x.shape[0]
            N = T * K
            C = 2 * N // E
            logits = jnp.einsum('th,eh->te', x.astype(jnp.float32), gate_w.astype(jnp.float32))
            scores = jax.nn.softmax(logits, axis=-1)
            topk_w, topk_ids = jax.lax.top_k(scores, K)
            topk_w = topk_w / jnp.sum(topk_w, axis=-1, keepdims=True)
            flat_ids = topk_ids.reshape(-1)
            flat_w = topk_w.reshape(-1)
            order = jnp.argsort(flat_ids)
            sorted_eid = flat_ids[order]
            tok = order // K
            counts = jnp.zeros((E,), jnp.int32).at[flat_ids].add(1)
            starts = jnp.cumsum(counts) - counts
            pos = jnp.arange(N) - starts[sorted_eid]
            buf = jnp.zeros((E, C, x.shape[1]), x.dtype).at[sorted_eid, pos].set(x[tok], mode='drop')
            gu = jnp.einsum('ech,ehf->ecf', buf, w13)
            g, u = jnp.split(gu, 2, axis=-1)
            act = jax.nn.silu(g) * u
            eo = jnp.einsum('eci,eih->ech', act, w2)
            out_slots = eo[sorted_eid, pos]
            routed = jnp.zeros_like(x).at[tok].add(out_slots * flat_w[order][:, None])
            return routed
        key = jax.random.key(seed)
        ks = jax.random.split(key, 8)
        s = 1.0 / np.sqrt(H)
        si = 1.0 / np.sqrt(I)
        return {'hidden_states': jax.random.normal(ks[0], (1, 512, H), jnp.float32), 'norm_w': jnp.ones((H,), jnp.float32), 'gate_w': jax.random.normal(ks[1], (E, H), jnp.float32) * s, 'w13': jax.random.normal(ks[2], (E, H, 2 * I), jnp.float32) * s, 'w2': jax.random.normal(ks[3], (E, I, H), jnp.float32) * si, 'shared_gate_w': jax.random.normal(ks[4], (H, I * N_SHARED), jnp.float32) * s, 'shared_up_w': jax.random.normal(ks[5], (H, I * N_SHARED), jnp.float32) * s, 'shared_down_w': jax.random.normal(ks[6], (I * N_SHARED, H), jnp.float32) * si}
    _L1_ffn_in = _L1_ffn_setup()
    _L1_c = _w((lambda *s: np.random.randn(*s).astype(np.float32) * 0.05)(4, 256))
    _L1_wmod = _w((lambda *s: np.random.randn(*s).astype(np.float32) * 0.05)(256, 6 * 256) * 256 ** (-0.5))
    _d = {'L0_attn_x': _L0_attn_in['x'], 'L0_attn_Wq': _L0_attn_in['Wq'], 'L0_attn_Wk': _L0_attn_in['Wk'], 'L0_attn_Wv': _L0_attn_in['Wv'], 'L0_attn_Wz': _L0_attn_in['Wz'], 'L0_attn_Wa': _L0_attn_in['Wa'], 'L0_attn_Wb': _L0_attn_in['Wb'], 'L0_attn_conv_q_w': _L0_attn_in['conv_q_w'], 'L0_attn_conv_k_w': _L0_attn_in['conv_k_w'], 'L0_attn_conv_v_w': _L0_attn_in['conv_v_w'], 'L0_attn_norm_w': _L0_attn_in['norm_w'], 'L0_attn_Wout': _L0_attn_in['Wout'], 'L0_ffn_lut': _L0_ffn_in['lut'], 'L0_ffn_gate_idx': _L0_ffn_in['gate_idx'], 'L0_ffn_up_idx': _L0_ffn_in['up_idx'], 'L0_ffn_down_idx': _L0_ffn_in['down_idx'], 'L0_c': _L0_c, 'L0_wmod': _L0_wmod, 'L1_attn_wq_codes': _L1_attn_in['wq_codes'], 'L1_attn_wq_scales': _L1_attn_in['wq_scales'], 'L1_attn_bq': _L1_attn_in['bq'], 'L1_attn_wk_codes': _L1_attn_in['wk_codes'], 'L1_attn_wk_scales': _L1_attn_in['wk_scales'], 'L1_attn_bk': _L1_attn_in['bk'], 'L1_attn_wv_codes': _L1_attn_in['wv_codes'], 'L1_attn_wv_scales': _L1_attn_in['wv_scales'], 'L1_attn_bv': _L1_attn_in['bv'], 'L1_attn_wo_codes': _L1_attn_in['wo_codes'], 'L1_attn_wo_scales': _L1_attn_in['wo_scales'], 'L1_attn_bo': _L1_attn_in['bo'], 'L1_ffn_norm_w': _L1_ffn_in['norm_w'], 'L1_ffn_gate_w': _L1_ffn_in['gate_w'], 'L1_ffn_w13': _L1_ffn_in['w13'], 'L1_ffn_w2': _L1_ffn_in['w2'], 'L1_ffn_shared_gate_w': _L1_ffn_in['shared_gate_w'], 'L1_ffn_shared_up_w': _L1_ffn_in['shared_up_w'], 'L1_ffn_shared_down_w': _L1_ffn_in['shared_down_w'], 'L1_c': _L1_c, 'L1_wmod': _L1_wmod}
    _x0 = _d['L0_attn_x']
    _d['L0_attn_x'] = jax.random.normal(jax.random.fold_in(jax.random.key(seed), 1), (4, 256, 256), dtype=_x0.dtype)
    del _x0
    return _d

def reference(L0_attn_x, L0_attn_Wq, L0_attn_Wk, L0_attn_Wv, L0_attn_Wz, L0_attn_Wa, L0_attn_Wb, L0_attn_conv_q_w, L0_attn_conv_k_w, L0_attn_conv_v_w, L0_attn_norm_w, L0_attn_Wout, L0_ffn_lut, L0_ffn_gate_idx, L0_ffn_up_idx, L0_ffn_down_idx, L0_c, L0_wmod, L1_attn_wq_codes, L1_attn_wq_scales, L1_attn_bq, L1_attn_wk_codes, L1_attn_wk_scales, L1_attn_bk, L1_attn_wv_codes, L1_attn_wv_scales, L1_attn_bv, L1_attn_wo_codes, L1_attn_wo_scales, L1_attn_bo, L1_ffn_norm_w, L1_ffn_gate_w, L1_ffn_w13, L1_ffn_w2, L1_ffn_shared_gate_w, L1_ffn_shared_up_w, L1_ffn_shared_down_w, L1_c, L1_wmod):

    def _L0_attn_ref(x, Wq, Wk, Wv, Wz, Wa, Wb, conv_q_w, conv_k_w, conv_v_w, norm_w, Wout):
        import jax, jax.numpy as jnp
        import numpy as np
        B, S, HID = (2, 256, 256)
        H, D, K = (16, 128, 4)
        ROPE_BASE = 1000000.0
        EPS_NORM = 1e-06

        def _silu(u):
            return u * jax.nn.sigmoid(u)

        def _causal_dwconv(x_bsc, w_ck):
            C, Kw = w_ck.shape
            y = jax.lax.conv_general_dilated(x_bsc.transpose(0, 2, 1), w_ck[:, None, :], (1,), [(Kw - 1, 0)], dimension_numbers=('NCH', 'OIH', 'NCH'), feature_group_count=C)
            return y.transpose(0, 2, 1)

        def _lag(u, s):
            if s == 0:
                return u
            pad = [(0, 0), (s, 0)] + [(0, 0)] * (u.ndim - 2)
            return jnp.pad(u, pad)[:, :u.shape[1]]
        Bc, Sc, _ = x.shape
        q = _silu(x @ Wq)
        k = _silu(x @ Wk)
        v = _silu(x @ Wv)
        z = x @ Wz
        a = x @ Wa
        b = x @ Wb
        q = _causal_dwconv(q, conv_q_w)
        k = _causal_dwconv(k, conv_k_w)
        v = _causal_dwconv(v, conv_v_w)
        q = q.reshape(Bc, Sc, H, D)
        k = k.reshape(Bc, Sc, H, D)
        v = v.reshape(Bc, Sc, H, D)
        inv = 1.0 / ROPE_BASE ** (jnp.arange(0, D, 2, dtype=jnp.float32) / D)
        fr = jnp.arange(Sc, dtype=jnp.float32)[:, None] * inv[None, :]
        cos = jnp.concatenate([jnp.cos(fr), jnp.cos(fr)], -1)[None, :, None, :]
        sin = jnp.concatenate([jnp.sin(fr), jnp.sin(fr)], -1)[None, :, None, :]

        def rot_half(u):
            u1, u2 = jnp.split(u, 2, axis=-1)
            return jnp.concatenate([-u2, u1], axis=-1)
        q = q * cos + rot_half(q) * sin
        k = k * cos + rot_half(k) * sin
        q = q / jnp.maximum(jnp.linalg.norm(q, axis=-1, keepdims=True), 1e-12)
        k = k / jnp.maximum(jnp.linalg.norm(k, axis=-1, keepdims=True), 1e-12)
        scale = 1.0 / D ** 0.5
        out = jnp.zeros_like(v)
        for s in range(K):
            k_s = _lag(k, s)
            v_s = _lag(v, s)
            a_s = _lag(a, s)
            attn = jnp.einsum('bshd,bshd->bsh', q, k_s) * scale
            gate = jax.nn.sigmoid(a_s * b)
            out = out + (attn * gate)[..., None] * v_s
        out = out.reshape(Bc, Sc, H * D)
        rms = jax.lax.rsqrt(jnp.mean(out * out, axis=-1, keepdims=True) + EPS_NORM)
        out = out * rms * norm_w * _silu(z)
        return out @ Wout

    def _L0_ffn_ref(x, lut, gate_idx, up_idx, down_idx):
        import jax, jax.numpy as jnp
        import numpy as np
        HIDDEN = 256
        INTER = 688
        LUT_SIZE = 16

        def _ghost_linear(x, idx, lut):
            w = lut[idx]
            return jnp.einsum('bsh,oh->bso', x, w)
        gate = _ghost_linear(x, gate_idx, lut)
        up = _ghost_linear(x, up_idx, lut)
        h = jax.nn.silu(gate) * up
        return _ghost_linear(h, down_idx, lut)

    def _L1_attn_ref(x, wq_codes, wq_scales, bq, wk_codes, wk_scales, bk, wv_codes, wv_scales, bv, wo_codes, wo_scales, bo):
        import jax, jax.numpy as jnp
        import numpy as np
        BLOCK = 32
        NUM_HEADS = 16
        HEAD_DIM = 128
        FP4_GRID = jnp.array([0.0, 0.5, 1.0, 1.5, 2.0, 3.0, 4.0, 6.0], dtype=jnp.float32)

        def quantize_to_mxfp4(w, block_size=BLOCK):
            D, F = w.shape
            blocks = w.reshape(D // block_size, block_size, F)
            amax = jnp.max(jnp.abs(blocks), axis=1)
            e = jnp.floor(jnp.log2(jnp.maximum(amax, 1e-12) / 6.0))
            scale = jnp.exp2(e)
            v = blocks / scale[:, None, :]
            idx = jnp.argmin(jnp.abs(jnp.abs(v)[..., None] - FP4_GRID), axis=-1)
            codes = jnp.sign(v) * FP4_GRID[idx]
            return (codes.reshape(D, F).astype(jnp.float32), scale.astype(jnp.float32))

        def _mxfp4_matmul(x, codes, scales, block_size=BLOCK):
            w = codes * jnp.repeat(scales, block_size, axis=0)
            return x @ w
        B, S, D = x.shape
        q = _mxfp4_matmul(x, wq_codes, wq_scales) + bq
        k = _mxfp4_matmul(x, wk_codes, wk_scales) + bk
        v = _mxfp4_matmul(x, wv_codes, wv_scales) + bv
        q = q.reshape(B, S, NUM_HEADS, HEAD_DIM)
        k = k.reshape(B, S, NUM_HEADS, HEAD_DIM)
        v = v.reshape(B, S, NUM_HEADS, HEAD_DIM)
        scores = jnp.einsum('bqhd,bkhd->bhqk', q, k) / jnp.sqrt(jnp.float32(HEAD_DIM))
        attn = jax.nn.softmax(scores, axis=-1)
        out = jnp.einsum('bhqk,bkhd->bqhd', attn, v).reshape(B, S, NUM_HEADS * HEAD_DIM)
        return _mxfp4_matmul(out, wo_codes, wo_scales) + bo

    def _L1_ffn_ref(hidden_states, norm_w, gate_w, w13, w2, shared_gate_w, shared_up_w, shared_down_w):
        import jax, jax.numpy as jnp
        import numpy as np
        H = 256
        I = 128
        E = 32
        K = 4
        N_SHARED = 1
        EPS = 1e-06

        def _rmsnorm(x, w, eps=EPS):
            var = jnp.mean(jnp.square(x), axis=-1, keepdims=True)
            return x * jax.lax.rsqrt(var + eps) * w

        def _moe_core(x, gate_w, w13, w2):
            T = x.shape[0]
            N = T * K
            C = 2 * N // E
            logits = jnp.einsum('th,eh->te', x.astype(jnp.float32), gate_w.astype(jnp.float32))
            scores = jax.nn.softmax(logits, axis=-1)
            topk_w, topk_ids = jax.lax.top_k(scores, K)
            topk_w = topk_w / jnp.sum(topk_w, axis=-1, keepdims=True)
            flat_ids = topk_ids.reshape(-1)
            flat_w = topk_w.reshape(-1)
            order = jnp.argsort(flat_ids)
            sorted_eid = flat_ids[order]
            tok = order // K
            counts = jnp.zeros((E,), jnp.int32).at[flat_ids].add(1)
            starts = jnp.cumsum(counts) - counts
            pos = jnp.arange(N) - starts[sorted_eid]
            buf = jnp.zeros((E, C, x.shape[1]), x.dtype).at[sorted_eid, pos].set(x[tok], mode='drop')
            gu = jnp.einsum('ech,ehf->ecf', buf, w13)
            g, u = jnp.split(gu, 2, axis=-1)
            act = jax.nn.silu(g) * u
            eo = jnp.einsum('eci,eih->ech', act, w2)
            out_slots = eo[sorted_eid, pos]
            routed = jnp.zeros_like(x).at[tok].add(out_slots * flat_w[order][:, None])
            return routed
        B, S, Hd = hidden_states.shape
        residual = hidden_states
        h = _rmsnorm(hidden_states, norm_w)
        x = h.reshape(-1, Hd)
        routed = _moe_core(x, gate_w, w13, w2)
        shared = jax.nn.silu(x @ shared_gate_w) * (x @ shared_up_w) @ shared_down_w
        out = residual + (routed + shared).reshape(B, S, Hd)
        return out
    x = L0_attn_x
    mod = (_silu(L0_c) @ L0_wmod).reshape(L0_c.shape[0], 6, 1, -1)
    sa, ca, ga, sb, cb, gb = (mod[:, 0], mod[:, 1], mod[:, 2], mod[:, 3], mod[:, 4], mod[:, 5])
    ga = (2 * (ga >= 0) - 1) * jnp.maximum(jnp.abs(ga), 0.25)
    gb = (2 * (gb >= 0) - 1) * jnp.maximum(jnp.abs(gb), 0.25)
    h = _layernorm(x, axis=-1) * (1 + ca) + sa
    x = x + ga * _L0_attn_ref(h, L0_attn_Wq, L0_attn_Wk, L0_attn_Wv, L0_attn_Wz, L0_attn_Wa, L0_attn_Wb, L0_attn_conv_q_w, L0_attn_conv_k_w, L0_attn_conv_v_w, L0_attn_norm_w, L0_attn_Wout)
    h = _layernorm(x, axis=-1) * (1 + cb) + sb
    x = x + gb * _L0_ffn_ref(h, L0_ffn_lut, L0_ffn_gate_idx, L0_ffn_up_idx, L0_ffn_down_idx)
    mod = (_silu(L1_c) @ L1_wmod).reshape(L1_c.shape[0], 6, 1, -1)
    sa, ca, ga, sb, cb, gb = (mod[:, 0], mod[:, 1], mod[:, 2], mod[:, 3], mod[:, 4], mod[:, 5])
    ga = (2 * (ga >= 0) - 1) * jnp.maximum(jnp.abs(ga), 0.25)
    gb = (2 * (gb >= 0) - 1) * jnp.maximum(jnp.abs(gb), 0.25)
    h = _layernorm(x, axis=-1) * (1 + ca) + sa
    x = x + ga * _L1_attn_ref(h, L1_attn_wq_codes, L1_attn_wq_scales, L1_attn_bq, L1_attn_wk_codes, L1_attn_wk_scales, L1_attn_bk, L1_attn_wv_codes, L1_attn_wv_scales, L1_attn_bv, L1_attn_wo_codes, L1_attn_wo_scales, L1_attn_bo)
    h = _layernorm(x, axis=-1) * (1 + cb) + sb
    x = x + gb * _L1_ffn_ref(h, L1_ffn_norm_w, L1_ffn_gate_w, L1_ffn_w13, L1_ffn_w2, L1_ffn_shared_gate_w, L1_ffn_shared_up_w, L1_ffn_shared_down_w)
    return x

_drawn_inputs = setup_inputs


def setup_inputs(seed=0):
    import zlib

    import numpy as np

    out = dict(_drawn_inputs(seed))
    spreads = {'L0_attn_norm_w': (1.0, 0.6),
     'L1_attn_bq': (0.0, 0.8),
     'L1_attn_bk': (0.0, 2.0),
     'L1_attn_bv': (0.0, 0.284),
     'L1_attn_bo': (0.0, 2.0),
     'L1_ffn_norm_w': (1.0, 0.6)}
    factors = {'L0_attn_Wq': 8.0,
     'L0_attn_Wk': 8.0,
     'L0_attn_Wv': 8.0,
     'L0_attn_Wz': 8.0,
     'L0_attn_Wa': 8.0,
     'L0_attn_Wb': 8.0,
     'L0_attn_conv_q_w': 8.0,
     'L0_attn_conv_k_w': 8.0,
     'L0_attn_conv_v_w': 8.0,
     'L0_attn_Wout': 8.0,
     'L0_ffn_lut': 4.645,
     'L0_c': 4.602,
     'L0_wmod': 4.457,
     'L1_attn_wq_codes': 2.98,
     'L1_attn_wq_scales': 8.0,
     'L1_attn_wk_codes': 2.928,
     'L1_attn_wk_scales': 8.0,
     'L1_attn_wv_scales': 8.0,
     'L1_attn_wo_scales': 4.798,
     'L1_ffn_gate_w': 6.017,
     'L1_ffn_w13': 5.685,
     'L1_ffn_w2': 5.666,
     'L1_ffn_shared_gate_w': 3.339,
     'L1_ffn_shared_up_w': 3.073,
     'L1_ffn_shared_down_w': 3.091}
    for name, (base, spread) in spreads.items():
        noise = np.random.default_rng([zlib.crc32(name.encode()), seed]).standard_normal(out[name].shape)
        drawn = base * np.exp(spread * noise) if base else spread * noise
        out[name] = jnp.asarray(drawn.astype(out[name].dtype))
    for name, factor in factors.items():
        out[name] = (out[name] * factor).astype(out[name].dtype)
    return out
```

```python
from contextlib import ExitStack

import concourse.bass as bass
from concourse import mybir

ALU = mybir.AluOpType
ACT = mybir.ActivationFunctionType
AX = mybir.AxisListType
F32 = mybir.dt.float32
I32 = mybir.dt.int32
U32 = mybir.dt.uint32

P = 128
B, S, D = 4, 256, 256
T = B * S
KC = D // P
NT = T // P
H, HD, TAPS = 16, 128, 4
PAD = TAPS - 1
BAND = T + B * PAD
INTER, LUT = 688, 16
MT = -(-INTER // P)
UPC = KC * INTER
LUTC = 2 * UPC + MT * D
LW = LUTC // H
LTURN = LUT // 2
LPRE = 4 * LW
E, TOPK, CAP = 32, 4, 256
NE = E + 1
QKV = 3 * KC * P
EW = 3 * D
SCALE = float(HD) ** -0.5
assert LW * H == LUTC and HD == P

C_ID, C_ONE, C_INV, C_STRICT, C_MASK, C_SEAM, C_COS, C_SIN, C_IOTA, C_TOK = 0, 128, 256, 384, 512, 640, 643, 899, 1155, 1187
C_SEL = 1195
C_ALL = C_SEL + 4 * NT - 1
M_CW, M_NW, M_WA, M_WB, M_BQKV, M_BO, M_RMS, M_GW = 0, 192, 208, 240, 272, 320, 322, 324
M_ALL = 324 + KC * E


def build(nc, a, out, b_rows, code_rows):
    ctx = ExitStack()
    named = {}

    def sg(name):
        if name not in named:
            named[name] = ctx.enter_context(nc.semaphore(name))
        return named[name]

    def norm(tag, step):
        order = [t for t in ("n0", "r0", "n1", "n2", "n3", "n4")
                 if t not in {"mean": "r0 n4", "centred": "r0 n4", "scaled": "r0 n4", "out": "r0 n4", "sq": "r0", "var": "r0", "rows": "r0", "rows_sb": "r0"}
                 .get(step, "").split()]
        return sg("norm_" + step), order.index(tag) + 1

    def sb(name, cols, dt=F32):
        return ctx.enter_context(nc.sbuf_tensor(name, [P, cols], dt))[:, :]

    with ctx:
        psum = ctx.enter_context(nc.psum_tensor("psum", [P, 8 * 512], F32))[:, :]

        def bank(i, n=512):
            return psum[:, i * 512:i * 512 + n]

        x_t, h_t, G = sb("x_t", KC * T), sb("h_t", KC * T), sb("G", H * T)
        cst, par_in = sb("cst", C_ALL), sb("par_in", M_ALL)
        lut_w = sb("lut_w", LUTC)
        ident, ones, inv_d = cst[:, C_ID:C_ID + P], cst[:, C_ONE:C_ONE + P], cst[:, C_INV:C_INV + P]
        strict, mask, seam = cst[:, C_STRICT:C_STRICT + P], cst[:, C_MASK:C_MASK + P], cst[:, C_SEAM:C_SEAM + PAD]
        cos_t, sin_t = cst[:, C_COS:C_COS + S], cst[:, C_SIN:C_SIN + S]
        iota_e, tok_id = cst[:, C_IOTA:C_IOTA + E], cst[:, C_TOK:C_TOK + NT]
        small = sb("small", 680)
        used = [0]

        def few(n):
            v = small[:, used[0]:used[0] + n]
            used[0] += n
            assert used[0] <= 640
            return v

        mod = [few(6 * KC * B), few(6 * KC * B)]
        msgn, mabs = few(6 * KC * B), few(6 * KC * B)
        stat, rstd, neg_half = few(NT), few(NT), few(2 * NT)
        ct = [few(KC * B), few(KC * B)]
        a_tok, a_head = few(H * NT), few(NT)
        ssq_s, rqk0, rqk1 = few(2 * NT), few(2 * NT), few(2 * NT)
        rqk = [rqk0, rqk1]
        ss_all = few(H * NT)
        nmax, rsum, rinv = few(8), few(8), few(8)
        lut = few(LUT)
        a_star = few(2)
        ARENA = 25472
        arena = sb("arena", ARENA)

        def carve(*sizes, base=0):
            o, v = base, []
            for n in sizes:
                v.append(arena[:, o:o + n])
                o += n
            assert o <= ARENA, o
            return v

        UW = B * (S + PAD)
        (uq, uk, uv, cq, ck, cv0, cv1, swq, swk, qr, kr, sqq, sqk, sz0, sz1, gate, gm, A, v_tok, junk,
         wh0, wh1, lidx, lt_all, lacc, rows_sb) = carve(
            UW, UW, UW, T, T, T, T, T, T, T, T, T, T, T, T, BAND, BAND, BAND, T, T,
            4 * KC * P, 4 * KC * P, LW, LTURN * LW, LW, P)
        u, c_ = {"q": uq, "k": uk, "v": uv}, {"q": cq, "k": ck}
        sw, rot, sqr = {"q": swq, "k": swk}, {"q": qr, "k": kr}, {"q": sqq, "k": sqk}
        cv, sz, wh = [cv0, cv1], [sz0, sz1], [wh0, wh1]
        lt = [lt_all[:, j * LW:j * LW + LW] for j in range(LTURN)]
        lidx_i = lidx.bitcast(I32)
        wmod = [G[:, 0:KC * 6 * D], G[:, KC * 6 * D:2 * KC * 6 * D]]
        b_sb = G[0:H, 2 * KC * 6 * D:2 * KC * 6 * D + T]

        (pre_idx, pre_tmp) = carve(LPRE, LUT * LPRE, base=5 * T)
        (post_idx, post_tmp) = carve(LPRE, LPRE, base=9 * T + H * D)
        ln_c, ln_sq, ln_b, wout, rb, gsb, hsb0, hsb1 = carve(KC * T, KC * T, T, H * D, T, T, T, T)
        hsb = [hsb0, hsb1]
        (q0, q1, k0, k1, v0, v1, p0, p1, pt_all, code0, code1, scl0, scl1, w10, w11, wo_c, wo_s) = carve(
            T, T, T, T, T, T, 512, 512, 4 * 512, QKV, QKV, QKV, QKV, QKV, QKV, H * D, H * D)
        q_sb, k_sb, v_sb, prob, code, scl, w1 = [q0, q1], [k0, k1], [v0, v1], [p0, p1], [code0, code1], [scl0, scl1], [w10, w11]
        (xr, we0, we1, cb0, cb1, sg0, sg1, aa0, aa1, ov, code_t, oh, lg, ex, mk, eqs, pos, tot, m8, mi, mif) = carve(
            KC * T, EW, EW, T, T, T, T, T, T, T, T, NT * E, NT * E, NT * E, NT * E, NT * E, NT * E, NT * E,
            NT * 8, NT * 8, NT * 8, base=5 * T)
        we, code_b, sgl, aa = [we0, we1], [cb0, cb1], [sg0, sg1], [aa0, aa1]
        t_star = small[0:1, 640:640 + NE].bitcast(I32)

        def chunk(t, k):
            return t[:, k * T:(k + 1) * T]

        def by_batch(v):
            return v.rearrange("p (b s) -> p b s", b=B)

        def by_tile(v, n=P):
            return v.rearrange("p (i t) -> p i t", t=n)

        def over_cols(v, n):
            return v.unsqueeze(2).broadcast_to([P, v.shape[1], n])

        def over_tiles(v, n):
            return v.unsqueeze(1).broadcast_to([P, n, v.shape[1]])

        def modv(l, w, k, b):
            c = (w * KC + k) * B + b
            return mod[l][:, c:c + 1]

        SA, CA, GA, SB_, CB, GB = range(6)

        block = ctx.enter_context(nc.Block())

        def mean_pe(pe, tag):
            for n in range(2):
                for k in range(KC):
                    i = nc.tensor.matmul(bank(n), inv_d, x_t[:, k * T + n * 512:k * T + n * 512 + 512],
                                         start=(k == 0), stop=(k == KC - 1))
            i.then_inc(norm(tag, "mean")[0], 1)

        def select(i):
            return cst[:, C_SEL + 2 * NT - 1 - i:C_SEL + 4 * NT - 1 - i]

        def var_pe(pe, tag):
            pe.wait_ge(*norm(tag, "sq"))
            for t in range(NT):
                for k in range(KC):
                    i = nc.tensor.matmul(bank(2)[0:2 * NT, 0:P], select(t), ln_sq[:, k * T + t * P:k * T + t * P + P],
                                         start=(t == 0 and k == 0), stop=(t == NT - 1 and k == KC - 1))
            i.then_inc(norm(tag, "rows")[0], 1)
            pe.wait_ge(*norm(tag, "rows_sb"))
            nc.tensor.transpose(bank(3)[:, 0:2 * NT], ln_b[0:2 * NT, 0:P], ident[0:2 * NT, 0:2 * NT])\
                .then_inc(norm(tag, "var")[0], 1)

        def spread_pe(pe, tag):
            pe.wait_ge(*norm(tag, "diag"))
            for n in range(2):
                i = nc.tensor.matmul(bank(4 + n), ones, ln_b[:, n * 512:n * 512 + 512], start=True, stop=True)
            i.then_inc(norm(tag, "spread")[0], 1)

        def square_act(act, tag, src, ready):
            act.wait_ge(*norm(*ready))
            nc.scalar.activation(ln_sq, src, ACT.Square).then_inc(norm(tag, "sq")[0], 1)

        def centre_dve(dve, tag):
            dve.wait_ge(*norm(tag, "mean"))
            for k in range(KC):
                i = nc.vector.tensor_tensor(chunk(ln_c, k), chunk(x_t, k), psum[:, 0:T], ALU.subtract)
            i.then_inc(norm(tag, "centred")[0], 1)

        def stat_dve(dve, tag, eps):
            dve.wait_ge(*norm(tag, "rows"))
            nc.vector.tensor_copy(ln_b[0:2 * NT, 0:P], bank(2)[0:2 * NT, 0:P]).then_inc(norm(tag, "rows_sb")[0], 1)
            dve.wait_ge(*norm(tag, "var"))
            nc.vector.tensor_scalar(stat, bank(3)[:, 0:NT], 1.0 / D, eps, ALU.mult, ALU.add).then_inc(norm(tag, "stat")[0], 1)

        def diag_dve(dve, tag):
            dve.wait_ge(*norm(tag, "rstd"))
            nc.vector.tensor_tensor(by_tile(ln_b), over_tiles(ident, NT), over_cols(rstd, P), ALU.mult)\
                .then_inc(norm(tag, "diag")[0], 1)

        def rstd_pool(pool, tag):
            pool.wait_ge(*norm(tag, "stat"))
            nc.gpsimd.tensor_tensor(rstd, stat, neg_half[:, 0:NT], ALU.pow).then_inc(norm(tag, "rstd")[0], 1)

        def modulate_dve(dve, tag, l, w_shift, w_scale):
            dve.wait_ge(*norm(tag, "spread"))
            for k in range(KC):
                i = nc.vector.tensor_tensor(chunk(ln_c, k), chunk(ln_c, k), psum[:, 4 * 512:4 * 512 + T], ALU.mult)
            i.then_inc(norm(tag, "scaled")[0], 1)
            dve.wait_ge(*norm(tag, "scaled"))
            for k in range(KC):
                for b in range(B):
                    c = slice(k * T + b * S, k * T + b * S + S)
                    i = nc.vector.tensor_scalar(h_t[:, c], ln_c[:, c], modv(l, w_scale, k, b), modv(l, w_shift, k, b),
                                                ALU.mult, ALU.add)
            i.then_inc(norm(tag, "out")[0], 1)

        def layer_norm_dve(dve, tag, l, w_shift, w_scale):
            centre_dve(dve, tag)
            stat_dve(dve, tag, 1e-5)
            diag_dve(dve, tag)
            modulate_dve(dve, tag, l, w_shift, w_scale)

        def layer_norm_pe(pe, tag):
            mean_pe(pe, tag)
            var_pe(pe, tag)
            spread_pe(pe, tag)

        def residual_dve(dve, done, l, w, y):
            for k in range(KC):
                for b in range(B):
                    c = slice(k * T + b * S, k * T + b * S + S)
                    i = nc.vector.scalar_tensor_tensor(x_t[:, c], y[:, c], modv(l, w, k, b), x_t[:, c], ALU.mult, ALU.add)
                if done == "y_out":
                    i.then_inc(sg(done), 1)
            if done != "y_out":
                i.then_inc(sg(done), 1)

        def slot(i):
            return psum[:, i * T:i * T + T]

        def s_block(i):
            return psum[:, 4 * 512 + i * P:4 * 512 + i * P + P]

        def s_seam(b):
            return psum[:, 4 * 512 + T + b * PAD:4 * 512 + T + b * PAD + PAD]

        def turns0(eng, turn):
            turn(0, 0, 0, (1,))
            turn(1, 0, 1, (1, 2))
            with eng.Fori(1, H // 2) as i:
                turn(2 * i, i, 0, (1, 2, 3))
                turn(2 * i + 1, i, 1, (1, 2, 3))
            turn(H, H // 2, 0, (2, 3))
            turn(H + 1, H // 2, 1, (3,))

        def turns1(eng, turn):
            turn(0, 0, 0, (1,))
            turn(1, 0, 1, (1, 2))
            with eng.Fori(1, H // 2) as i:
                turn(2 * i, i, 0, (1, 2))
                turn(2 * i + 1, i, 1, (1, 2))
            turn(H, H // 2, 0, (2,))

        def since(h, n):
            return not isinstance(h, int) or h >= n

        def evens(h):
            return min(h + 1, H) if isinstance(h, int) else h + 1

        @block.sync
        def _(sp):
            sp.dma_start(ct[0], a["c0"]).then_inc(sg("in_c"), 16)
            sp.dma_start(ct[1], a["c1"]).then_inc(sg("in_c"), 16)
            sp.dma_start(x_t, a["x"]).then_inc(sg("in_x"), 16)
            sp.dma_start(cst, a["cst"]).then_inc(sg("in_cst"), 16)
            sp.dma_start(wmod[0], a["wmod0"]).then_inc(sg("in_wmod0"), 16)
            sp.dma_start(wmod[1], a["wmod1"]).then_inc(sg("in_wmod1"), 16)
            sp.dma_start(par_in, a["par_in"]).then_inc(sg("in_par"), 16)
            sp.dma_start(lut, a["lut"].broadcast_to([P, LUT])).then_inc(sg("in_lut"), 16)
            sp.dma_start(pre_idx.bitcast(I32), a["idx_pre"]).then_inc(sg("idx_pre"), 16)
            sp.wait_ge(*norm("n0", "out"))
            sp.wait_ge(sg("lut_pre"), LUT - 1)
            sp.dma_start(lidx_i, a["idx"][0]).then_inc(sg("a0_idx"), 16)
            for par in range(2):
                sp.dma_start(wh[par], a["w_qkvz"][par]).then_inc(sg(f"a0_w{par}"), 16)
            sp.wait_ge(sg("b_sb"), 1)
            sp.dma_start(b_rows, b_sb).then_inc(sg("b_rows"), 16)
            sp.wait_ge(sg("b_rows"), 16)

            def lut_out(h, hh):
                sp.wait_ge(sg("a0_lut_add"), LTURN * (h + 1))
                sp.dma_start(lut_w[:, bass.ds(LPRE + hh * LW, LW)], lacc).then_inc(sg("a0_lut_out"), 16)

            def turn(h, hh, par, ahead):
                if since(h, 1):
                    sp.wait_ge(sg("a0_gm"), h)
                sp.dma_start(gate[:, 0:T], b_rows[bass.ds(h, 1), :].broadcast_to([P, T])).then_inc(sg("a0_b"), 16)
                for s in "qk":
                    if since(h, 1):
                        sp.wait_ge(sg("a0_rope_" + s), h)
                    sp.wait_ge(sg("a0_conv_" + s), 3 * h + 3)
                    sp.dma_start(sw[s][0:64, :], c_[s][64:128, :]).then_inc(sg("a0_sw_" + s), 16)
                    sp.dma_start(sw[s][64:128, :], c_[s][0:64, :]).then_inc(sg("a0_sw_" + s), 16)
                if ahead:
                    sp.wait_ge(sg("a0_z"), h + 1)
                    sp.dma_start(wh[par], a["w_qkvz"][h + 2]).then_inc(sg(f"a0_w{par}"), 16)
                if par == 1:
                    lut_out(h, hh)
                    if ahead:
                        sp.wait_ge(sg("a0_lut_tmp"), LTURN * (h + 1))
                        sp.dma_start(lidx_i, a["idx"][hh + 1]).then_inc(sg("a0_idx"), 16)

            turn(0, 0, 0, True)
            turn(1, 0, 1, True)
            with sp.Fori(1, H // 2 - 1) as i:
                turn(2 * i, i, 0, True)
                turn(2 * i + 1, i, 1, True)
            turn(H - 2, H // 2 - 1, 0, False)
            turn(H - 1, H // 2 - 1, 1, False)
            sp.wait_ge(sg("a0_gT_sb"), H)
            sp.dma_start(post_idx.bitcast(I32), a["idx_post"]).then_inc(sg("idx_post"), 16)
            sp.dma_start(wout, a["w_out"]).then_inc(sg("in_wout"), 16)

            sp.wait_ge(*norm("n2", "out"))
            def load1(h, par):
                sp.dma_start(code[par], a["qkv_codes"][h]).then_inc(sg(f"a1_w{par}"), 16)
                for g in range(4):
                    sp.dma_start(scl[par][32 * g:32 * g + 32, :], a["qkv_scales"][h][g:g + 1, :].broadcast_to([32, QKV]))\
                        .then_inc(sg(f"a1_w{par}"), 16)

            load1(0, 0)
            load1(1, 1)
            sp.dma_start(wo_c, a["wo_codes"]).then_inc(sg("in_wo"), 16)
            for g in range(4):
                sp.dma_start(wo_s[32 * g:32 * g + 32, :], a["wo_scales"][g:g + 1, :].broadcast_to([32, H * D]))\
                    .then_inc(sg("in_wo"), 16)
            with sp.Fori(0, H // 2 - 1) as i:
                for par in range(2):
                    sp.wait_ge(sg("a1_wmul"), 2 * i + par + 1)
                    load1(2 * i + par + 2, par)

            sp.wait_ge(sg("moe_codeT"), 1)
            sp.dma_start(code_rows, code_t[0:NE, :]).then_inc(sg("code_rows"), 16)

            def load_up(e, par):
                sp.dma_start(we[par][:, 0:2 * D], a["w_moe"][e][:, 0:2 * D]).then_inc(sg(f"moe_w13_{par}"), 16)

            def load_down(e, par):
                sp.dma_start(we[par][:, 2 * D:EW], a["w_moe"][e][:, 2 * D:EW]).then_inc(sg(f"moe_w2_{par}"), 16)

            for e in range(2):
                load_up(e, e)
                load_down(e, e)
            sp.wait_ge(sg("code_rows"), 16)
            for e in range(2):
                sp.dma_start(code_b[e], code_rows[e:e + 1, :].broadcast_to([P, T])).then_inc(sg(f"moe_c{e}"), 16)

            def load_e(e, par):
                sp.wait_ge(sg("moe_u"), e - 1)
                load_up(e, par)
                sp.wait_ge(sg("moe_act"), 2 * (e - 1))
                sp.dma_start(code_b[par], code_rows[bass.ds(e, 1), :].broadcast_to([P, T])).then_inc(sg(f"moe_c{par}"), 16)
                sp.wait_ge(sg("moe_down"), e - 1)
                load_down(e, par)

            with sp.Fori(1, NE // 2) as i:
                load_e(2 * i, 0)
                load_e(2 * i + 1, 1)
            load_e(NE - 1, 0)
            for k in range(KC):
                sp.wait_ge(sg("y_out"), k + 1)
                sp.dma_start(out[:, k * T:(k + 1) * T], chunk(x_t, k)).then_inc(sg("out_written"), 16)
            sp.wait_ge(sg("out_written"), 16 * KC)

        @block.tensor
        def _(pe):
            def modulation(l):
                pe.wait_ge(sg("silu_c"), 2)
                pe.wait_ge(sg(f"in_wmod{l}"), 16)
                for f in range(6 * KC):
                    for k in range(KC):
                        i = nc.tensor.matmul(bank(6 + l)[:, f * B:f * B + B],
                                             wmod[l][:, k * 6 * D + f * P:k * 6 * D + f * P + P],
                                             ct[l][:, k * B:k * B + B], start=(k == 0), stop=(k == KC - 1))
                i.then_inc(sg("mod_ps"), 1)

            pe.wait_ge(sg("in_x"), 16)
            pe.wait_ge(sg("in_cst"), 16)
            mean_pe(pe, "n0")
            modulation(0)
            var_pe(pe, "n0")
            modulation(1)
            spread_pe(pe, "n0")
            pe.wait_ge(*norm("n0", "out"))
            pe.wait_ge(sg("in_par"), 16)
            for t in range(NT):
                for k in range(KC):
                    i = nc.tensor.matmul(bank(0)[:, t * H:t * H + H], h_t[:, k * T + t * P:k * T + t * P + P],
                                         par_in[:, M_WA + k * H:M_WA + k * H + H], start=(k == 0), stop=(k == KC - 1))
            for n in range(2):
                for k in range(KC):
                    i = nc.tensor.matmul(bank(2 + n)[0:H, :], par_in[:, M_WB + k * H:M_WB + k * H + H],
                                         h_t[:, k * T + n * 512:k * T + n * 512 + 512], start=(k == 0), stop=(k == KC - 1))
            i.then_inc(sg("ab_ps"), 1)
            pe.wait_ge(sg("a_sb"), 1)
            pe.wait_ge(sg("b_sb"), 1)

            def project(dst, w, rows, n_w=KC):
                for n in range(2):
                    for k in range(n_w):
                        i = nc.tensor.matmul(dst[0:rows, n * 512:n * 512 + 512], w(k),
                                             h_t[:, k * T + n * 512:k * T + n * 512 + 512],
                                             start=(k == 0), stop=(k == n_w - 1))
                return i

            def turn(h, hh, par, st):
                def w(j, k):
                    return wh[par][:, (j * KC + k) * P:(j * KC + k) * P + P]

                if 1 in st:
                    pe.wait_ge(sg(f"a0_w{par}"), 16 * (hh + 1))
                    if since(h, 1):
                        pe.wait_ge(sg("a0_silu_v"), h)
                    if since(h, 2):
                        pe.wait_ge(sg("a0_v_tok"), h - 1)
                    project(slot(0), lambda k: w(0, k), P).then_inc(sg("a0_q"), 1)
                if 2 in st:
                    pe.wait_ge(sg("a0_rows_sb"), h)
                    if since(h, 2):
                        pe.wait_ge(sg("a0_ssq_s"), h - 1)
                    nc.tensor.transpose(bank(7)[:, P:2 * P], rows_sb, ident)\
                        .then_inc(sg("a0_ssqT"), 1)
                if 3 in st:
                    pe.wait_ge(sg("a0_g"), h - 1)
                    pe.wait_ge(sg("a0_A"), h - 1)
                    for i in range(NT):
                        t = nc.tensor.transpose(s_block(i), sz[par][:, i * P:i * P + P], ident)
                    t.then_inc(sg("a0_gT"), 1)
                if 1 in st:
                    if since(h, 1):
                        pe.wait_ge(sg("a0_silu_z"), h)
                    if since(h, 2):
                        pe.wait_ge(sg("a0_g"), h - 1)
                        pe.wait_ge(sg("a0_sqo"), h - 1)
                    project(slot(1), lambda k: w(1, k), P).then_inc(sg("a0_k"), 1)
                    pe.wait_ge(sg("a0_silu_q"), h + 1)
                    project(slot(0), lambda k: w(2, k), P).then_inc(sg("a0_v"), 1)
                if 2 in st:
                    pe.wait_ge(sg("a0_rope_q"), h)
                    pe.wait_ge(sg("a0_rope_k"), h)
                    if since(h, 2):
                        pe.wait_ge(sg("a0_gT_sb"), h - 1)
                        pe.wait_ge(sg("a0_A"), h - 1)
                    for i in range(NT):
                        nc.tensor.matmul(s_block(i), kr[:, i * P:i * P + P], qr[:, i * P:i * P + P], start=True, stop=True)
                    for b in range(B):
                        i = nc.tensor.matmul(s_seam(b), kr[:, b * S:b * S + P], qr[:, b * S + P:b * S + P + PAD],
                                             start=True, stop=True)
                    i.then_inc(sg("a0_S"), 1)
                if 1 in st:
                    pe.wait_ge(sg("a0_silu_k"), h + 1)
                    for t in range(NT):
                        for k in range(KC):
                            i = nc.tensor.matmul(slot(1)[:, t * P:t * P + P], h_t[:, k * T + t * P:k * T + t * P + P],
                                                 w(3, k), start=(k == 0), stop=(k == KC - 1))
                    i.then_inc(sg("a0_z"), 1)
                if 2 in st:
                    pe.wait_ge(sg("a0_conv_v"), 3 * h)
                    pe.wait_ge(sg("a0_silu_v"), evens(h))
                    for i in range(NT):
                        t = nc.tensor.transpose(slot(0)[:, i * P:i * P + P], cv[1 - par][:, i * P:i * P + P], ident)
                    t.then_inc(sg("a0_vT"), 1)
                if 1 in st:
                    for j, s in enumerate("qk"):
                        pe.wait_ge(sg("a0_sq_" + s), h + 1)
                        if since(h, 1) and j == 0:
                            pe.wait_ge(sg("a0_ssq_s"), h)
                        for i in range(NT):
                            n = j * NT + i
                            m = nc.tensor.matmul(bank(7)[0:2 * NT, 0:P], select(n), sqr[s][:, i * P:i * P + P],
                                                 start=(n == 0), stop=(n == 2 * NT - 1))
                    m.then_inc(sg("a0_ssq"), 1)
                if 2 in st:
                    pe.wait_ge(sg("a0_A"), h)
                    pe.wait_ge(sg("a0_v_tok"), h)
                    pe.wait_ge(sg("a0_silu_z"), evens(h))
                    for i in range(NT):
                        o = slot(1)[:, i * P:i * P + P]
                        m = nc.tensor.matmul(o, A[:, i * P:i * P + P], v_tok[:, i * P:i * P + P], start=True, stop=(i % 2 == 0),
                                             skip_group_check=True)
                        if i % 2:
                            c = T + (i // 2) * PAD
                            m = nc.tensor.matmul(o[0:PAD, :], A[:, c:c + PAD], v_tok[:, (i - 1) * P:i * P], start=False,
                                                 stop=True, skip_group_check=True)
                    m.then_inc(sg("a0_o"), 1)

            turns0(pe, turn)
            pe.wait_ge(sg("in_wout"), 16)
            pe.wait_ge(sg("a0_gT_sb"), H)
            pe.wait_ge(sg("a0_sqo"), H)

            def out_project(w):
                for m in range(KC):
                    for n in range(2):
                        for h in range(H):
                            i = nc.tensor.matmul(bank(2 * m + n), w[:, h * D + m * P:h * D + m * P + P],
                                                 G[:, h * T + n * 512:h * T + n * 512 + 512], start=(h == 0), stop=(h == H - 1))
                return i

            out_project(wout).then_inc(sg("a0_out"), 1)
            spread_pe(pe, "r0")

            pe.wait_ge(sg("x1"), 1)
            layer_norm_pe(pe, "n1")
            pe.wait_ge(*norm("n1", "out"))
            pe.wait_ge(sg("lut_pre"), LUT - 1)
            pe.wait_ge(sg("a0_lut_out"), 16 * (H // 2))
            pe.wait_ge(sg("lut_post"), 2 * LUT - 1)
            def down(m):
                r = min(P, INTER - m * P)
                pe.wait_ge(sg("f_h"), m + 1)
                for o in range(KC):
                    for n in range(2):
                        i = nc.tensor.matmul(bank(4 + 2 * o + n), lut_w[0:r, 2 * UPC + m * D + o * P:2 * UPC + m * D + o * P + P],
                                             hsb[m % 2][0:r, n * 512:n * 512 + 512], start=(m == 0), stop=(m == MT - 1))
                i.then_inc(sg("f_down"), 1)

            for m in range(MT):
                r = min(P, INTER - m * P)
                if m:
                    pe.wait_ge(sg("f_silu"), m)
                project(slot(0), lambda k: lut_w[:, k * INTER + m * P:k * INTER + m * P + r], r).then_inc(sg("f_g"), 1)
                if m:
                    pe.wait_ge(sg("f_h"), m)
                project(slot(1), lambda k: lut_w[:, UPC + k * INTER + m * P:UPC + k * INTER + m * P + r], r)\
                    .then_inc(sg("f_u"), 1)
                if m:
                    down(m - 1)
            down(MT - 1)

            pe.wait_ge(sg("x2"), 1)
            layer_norm_pe(pe, "n2")
            pe.wait_ge(*norm("n2", "out"))

            def turn1(h, hh, par, st):
                old = 1 - par

                def w(j, k):
                    return w1[par][:, (j * KC + k) * P:(j * KC + k) * P + P]

                def scores(b):
                    if b < 2:
                        if since(h, 2):
                            pe.wait_ge(sg("a1_exp"), 4 * (h - 2) + b + 3)
                    else:
                        pe.wait_ge(sg("a1_exp"), 4 * (h - 1) + b - 1)
                    for i in range(2):
                        m = nc.tensor.matmul(bank(4 + b % 2)[:, i * S:i * S + S], q_sb[old][:, b * S + i * P:b * S + i * P + P],
                                             k_sb[old][:, b * S:b * S + S], start=True, stop=True)
                    m.then_inc(sg("a1_S"), 1)

                def turned(b):
                    pe.wait_ge(sg("a1_norm"), 4 * (h - 1) + b + 1)
                    if b < 2:
                        if since(h, 2):
                            pe.wait_ge(sg(("a1_pt_act", "a1_pt_dve")[b]), 2 * (h - 1))
                    else:
                        pe.wait_ge(sg(("a1_pt_act", "a1_pt_dve")[b - 2]), 2 * (h - 1) + 1)
                    for i in range(2):
                        for j in range(2):
                            t = nc.tensor.transpose(bank(6 + b % 2)[:, j * S + i * P:j * S + i * P + P],
                                                    prob[b % 2][:, i * S + j * P:i * S + j * P + P], ident)
                    t.then_inc(sg("a1_T"), 1)

                if 2 in st:
                    pe.wait_ge(sg("a1_q_sb"), h)
                    pe.wait_ge(sg("a1_k_sb"), h)
                    scores(0)
                    scores(1)
                if 1 in st:
                    pe.wait_ge(sg("a1_wmul"), h + 1)
                    if since(h, 1):
                        pe.wait_ge(sg("a1_v_sb"), h)
                    project(slot(0), lambda k: w(0, k), P).then_inc(sg("a1_q"), 1)
                if 2 in st:
                    turned(0)
                    scores(2)
                    turned(1)
                    scores(3)
                if 1 in st:
                    if since(h, 2):
                        pe.wait_ge(sg("a1_o_sb"), h - 1)
                    elif h == 1:
                        pe.wait_ge(sg("a1_k_sb"), 1)
                    project(slot(1), lambda k: w(1, k), P).then_inc(sg("a1_k"), 1)
                if 2 in st:
                    turned(2)
                if 1 in st:
                    pe.wait_ge(sg("a1_q_sb"), h + 1)
                    for t in range(NT):
                        for k in range(KC):
                            i = nc.tensor.matmul(slot(0)[:, t * P:t * P + P], h_t[:, k * T + t * P:k * T + t * P + P],
                                                 w(2, k), start=(k == 0), stop=(k == KC - 1))
                    i.then_inc(sg("a1_v"), 1)
                if 2 in st:
                    turned(3)
                    pe.wait_ge(sg("a1_k_sb"), evens(h))
                    pe.wait_ge(sg("a1_v_sb"), h)
                    pe.wait_ge(sg("a1_pt_act"), 2 * h)
                    pe.wait_ge(sg("a1_pt_dve"), 2 * h)
                    for b in range(B):
                        for j in range(2):
                            m = nc.tensor.matmul(slot(1)[:, b * S:b * S + S], v_sb[old][:, (2 * b + j) * P:(2 * b + j) * P + P],
                                                 pt_all[:, b * 512 + j * S:b * 512 + j * S + S], start=(j == 0), stop=(j == 1))
                    m.then_inc(sg("a1_o"), 1)

            turns1(pe, turn1)
            pe.wait_ge(sg("a1_womul"), 1)
            pe.wait_ge(sg("a1_o_sb"), H)
            out_project(wo_c).then_inc(sg("a1_out"), 1)

            pe.wait_ge(sg("x3"), 1)
            layer_norm_pe(pe, "n3")
            var_pe(pe, "n4")
            spread_pe(pe, "n4")
            pe.wait_ge(sg("xr"), 1)
            for t in range(NT):
                for k in range(KC):
                    i = nc.tensor.matmul(bank(0)[:, t * E:t * E + E], xr[:, k * T + t * P:k * T + t * P + P],
                                         par_in[:, M_GW + k * E:M_GW + k * E + E], start=(k == 0), stop=(k == KC - 1))
            i.then_inc(sg("moe_logits"), 1)
            pe.wait_ge(sg("moe_mask"), 1)
            nc.tensor.matmul(bank(1)[:, 0:NT * E], strict, mk, start=True, stop=True)
            nc.tensor.matmul(bank(2)[:, 0:NT * E], ones, mk, start=True, stop=True).then_inc(sg("moe_count"), 1)
            pe.wait_ge(sg("moe_oh"), 1)
            for t in range(NT):
                i = nc.tensor.matmul(bank(3)[0:1, 0:E], tok_id[:, t:t + 1], oh[:, t * E:t * E + E], start=(t == 0), stop=(t == NT - 1))
            i.then_inc(sg("moe_star_ps"), 1)
            pe.wait_ge(sg("moe_code"), 1)
            for t in range(NT):
                i = nc.tensor.transpose(psum[0:E, 4 * 512 + t * P:4 * 512 + t * P + P],
                                        ex[:, t * E:t * E + E], ident)
            i.then_inc(sg("moe_codeT_ps"), 1)
            pe.wait_ge(sg("moe_codeT"), 1)
            pe.wait_ge(sg("moe_star"), 1)

            def up_e(e, par, hh):
                pe.wait_ge(sg(f"moe_w13_{par}"), 16 * (hh + 1))
                for j, (ready, done) in enumerate((("moe_silu", "moe_g"), ("moe_gu", "moe_u"))):
                    if since(e, 1):
                        pe.wait_ge(sg(ready), e)
                    for n in range(2):
                        for k in range(KC):
                            i = nc.tensor.matmul(slot(j)[:, n * 512:n * 512 + 512], we[par][:, k * D + j * P:k * D + j * P + P],
                                                 xr[:, k * T + n * 512:k * T + n * 512 + 512], start=(k == 0), stop=(k == KC - 1))
                    i.then_inc(sg(done), 1)

            def down_e(e, par, hh, first=False, last=False):
                pe.wait_ge(sg(f"moe_w2_{par}"), 16 * (hh + 1))
                pe.wait_ge(sg("moe_act"), 2 * (e + 1))
                for m in range(KC):
                    for n in range(2):
                        i = nc.tensor.matmul(bank(4 + 2 * m + n), we[par][:, 2 * D + m * P:2 * D + m * P + P],
                                             aa[par][:, n * 512:n * 512 + 512], start=first, stop=last, skip_group_check=True)
                i.then_inc(sg("moe_down"), 1)

            up_e(0, 0, 0)
            up_e(1, 1, 0)
            down_e(0, 0, 0, first=True)
            with pe.Fori(1, NE // 2) as i:
                up_e(2 * i, 0, i)
                down_e(2 * i - 1, 1, i - 1)
                up_e(2 * i + 1, 1, i)
                down_e(2 * i, 0, i)
            up_e(NE - 1, 0, NE // 2)
            down_e(NE - 2, 1, NE // 2 - 1)
            down_e(NE - 1, 0, NE // 2, last=True)

        @block.scalar
        def _(act):
            act.wait_ge(sg("in_c"), 32)
            for l in range(2):
                nc.scalar.activation(ct[l], ct[l], ACT.Silu).then_inc(sg("silu_c"), 1)
            square_act(act, "n0", ln_c, ("n0", "centred"))
            act.wait_ge(sg("ab_ps"), 1)
            act.wait_ge(sg("mod_ps"), 2)
            nc.scalar.activation(b_sb, psum[0:H, 2 * 512:2 * 512 + T], ACT.Copy).then_inc(sg("b_sb"), 1)

            def turn(h, hh, par, st):
                def cw(w, j):
                    return par_in[:, bass.ds(M_CW + (w * H + h) * TAPS + j, 1)]

                def silu_and_tap(w, s, dst):
                    act.wait_ge(sg("a0_" + s), h + 1)
                    if since(h, 1):
                        act.wait_ge(sg("a0_conv_" + s), 3 * h)
                    nc.scalar.activation(by_batch(u[s])[:, :, PAD:PAD + S], by_batch(slot({"q": 0, "k": 1, "v": 0}[s])),
                                         ACT.Silu).then_inc(sg("a0_silu_" + s), 1)
                    act.wait_ge(sg("a0_silu_" + s), h + 1)
                    if s == "v":
                        if since(h, 2):
                            act.wait_ge(sg("a0_vT"), h - 1)
                    elif since(h, 1):
                        act.wait_ge(sg("a0_sw_" + s), 32 * h)
                        act.wait_ge(sg("a0_rc_" + s), h)
                        act.wait_ge(sg("a0_sq_" + s), h)
                    nc.scalar.activation(by_batch(dst), by_batch(u[s])[:, :, 0:S], ACT.Copy, scale=cw(w, 0))\
                        .then_inc(sg("a0_tap_" + s), 1)

                if 1 in st:
                    if not since(h, 1):
                        act.wait_ge(sg("pads"), 1)
                        act.wait_ge(sg("in_par"), 16)
                    silu_and_tap(0, "q", cq)
                if 3 in st:
                    act.wait_ge(sg("a0_gT"), h - 1)
                    nc.scalar.activation(G[:, bass.ds((h - 2) * T, T)], psum[:, 4 * 512:4 * 512 + T], ACT.Copy,
                                         scale=par_in[:, bass.ds(M_NW + h - 2, 1)]).then_inc(sg("a0_gT_sb"), 1)
                if 1 in st:
                    silu_and_tap(1, "k", ck)
                    silu_and_tap(2, "v", cv[par])
                    for s in "qk":
                        act.wait_ge(sg("a0_conv_" + s), 3 * h + 3)
                        if since(h, 1):
                            act.wait_ge(sg("a0_ssq"), h)
                        nc.scalar.activation(sqr[s], c_[s], ACT.Square).then_inc(sg("a0_sq_" + s), 1)
                    act.wait_ge(sg("a0_z"), h + 1)
                    if since(h, 2):
                        act.wait_ge(sg("a0_gT"), h - 1)
                    nc.scalar.activation(sz[par], slot(1), ACT.Silu).then_inc(sg("a0_silu_z"), 1)
                    act.wait_ge(sg("a0_ab"), h + 1)
                    nc.scalar.activation(gate, gate, ACT.Tanh, scale=0.5).then_inc(sg("a0_tanh"), 1)
                if 2 in st:
                    act.wait_ge(sg("a0_vT"), h)
                    if since(h, 2):
                        act.wait_ge(sg("a0_o"), h - 1)
                    act.wait_ge(sg("a0_rqk"), h)
                    for i in range(NT):
                        c = slice(i * P, i * P + P)
                        m = nc.scalar.activation(v_tok[:, c], slot(0)[:, c], ACT.Copy,
                                                 scale=rqk[1 - par][:, NT + i:NT + i + 1])
                    m.then_inc(sg("a0_v_tok"), 1)
                    act.wait_ge(sg("a0_o"), h)
                    if since(h, 2):
                        act.wait_ge(sg("a0_sqo"), h - 1)
                    for i in range(NT):
                        if i == NT // 2:
                            m.then_inc(sg("a0_sqo_lo"), 1)
                            act.wait_ge(sg("a0_g_hi"), h)
                        m = nc.scalar.activation(junk[:, i * P:i * P + P], slot(1)[:, i * P:i * P + P], ACT.Square, scale=rqk[1 - par][:, i:i + 1],
                                                 accum_out=ss_all[:, bass.ds((h - 1) * NT + i, 1)])
                    m.then_inc(sg("a0_sqo"), 1)

            turns0(act, turn)
            act.wait_ge(*norm("r0", "spread"))
            nc.scalar.activation(rb, psum[:, 4 * 512:4 * 512 + T], ACT.Copy).then_inc(sg("rms_sb"), 1)
            square_act(act, "n1", ln_c, ("n1", "centred"))
            for m in range(MT):
                r = min(P, INTER - m * P)
                act.wait_ge(sg("f_g"), m + 1)
                if m:
                    act.wait_ge(sg("f_h"), m)
                nc.scalar.activation(gsb[0:r, :], slot(0)[0:r, :], ACT.Silu).then_inc(sg("f_silu"), 1)
            square_act(act, "n2", ln_c, ("n2", "centred"))

            def turn1(h, hh, par, st):
                old = 1 - par

                def expo(b):
                    n = 4 * (h - 1) + b
                    act.wait_ge(sg("a1_nmax"), n + 1)
                    if b >= 2:
                        act.wait_ge(sg("a1_T"), n - 1)
                    elif since(h, 2):
                        act.wait_ge(sg("a1_T"), n - 1)
                    for i in range(2):
                        e = nc.scalar.activation(prob[b % 2][:, i * S:i * S + S], bank(4 + b % 2)[:, i * S:i * S + S], ACT.Exp,
                                                 bias=nmax[:, 2 * b + i:2 * b + i + 1], scale=SCALE,
                                                 accum_out=rsum[:, 2 * b + i:2 * b + i + 1])
                    e.then_inc(sg("a1_exp"), 1)

                def pt_out(b):
                    act.wait_ge(sg("a1_T"), 4 * (h - 1) + b + 1)
                    if since(h, 2):
                        act.wait_ge(sg("a1_o"), h - 1)
                    nc.scalar.activation(pt_all[:, b * 512:b * 512 + 512], bank(6 + b % 2), ACT.Copy).then_inc(sg("a1_pt_act"), 1)

                if 2 in st:
                    expo(0)
                    expo(1)
                if 1 in st:
                    act.wait_ge(sg("a1_q"), h + 1)
                    nc.scalar.activation(q_sb[par], slot(0), ACT.Identity, bias=par_in[:, bass.ds(M_BQKV + h, 1)])\
                        .then_inc(sg("a1_q_sb"), 1)
                if 2 in st:
                    pt_out(0)
                    expo(2)
                    expo(3)
                    pt_out(2)
                if 1 in st:
                    act.wait_ge(sg("a1_v"), h + 1)
                    if since(h, 2):
                        act.wait_ge(sg("a1_o"), h - 1)
                    nc.scalar.activation(v_sb[par], slot(0), ACT.Copy).then_inc(sg("a1_v_sb"), 1)

            act.wait_ge(*norm("n2", "out"))
            turns1(act, turn1)
            square_act(act, "n3", ln_c, ("n3", "centred"))
            square_act(act, "n4", h_t, ("n3", "out"))
            act.wait_ge(sg("moe_shifted"), 1)
            nc.scalar.activation(ex, lg, ACT.Exp).then_inc(sg("moe_exp"), 1)
            act.wait_ge(sg("moe_codeT_ps"), 1)
            act.wait_ge(sg("code_ones"), 1)
            nc.scalar.activation(code_t[0:E, :], psum[0:E, 4 * 512:4 * 512 + T], ACT.Copy).then_inc(sg("moe_codeT"), 1)

            def expert(e, par):
                act.wait_ge(sg("moe_g"), e + 1)
                if since(e, 2):
                    act.wait_ge(sg("moe_gu"), e - 1)
                nc.scalar.activation(sgl[par], slot(0), ACT.Silu).then_inc(sg("moe_silu"), 1)

            expert(0, 0)
            expert(1, 1)
            with act.Fori(1, NE // 2) as i:
                expert(2 * i, 0)
                expert(2 * i + 1, 1)
            expert(NE - 1, 0)

        @block.vector
        def _(dve):
            def modulation(l):
                dve.wait_ge(sg("mod_ps"), l + 1)
                n = KC * B
                done = sg(f"mod{l}")
                nc.vector.tensor_copy(mod[l], bank(6 + l)[:, 0:6 * n]).then_inc(done, 1)
                dve.wait_ge(done, 1)
                for w in (CA, CB):
                    nc.vector.tensor_scalar(mod[l][:, w * n:w * n + n], mod[l][:, w * n:w * n + n], 1.0, None, ALU.add)
                for w in (GA, GB):
                    g = slice(w * n, w * n + n)
                    nc.vector.tensor_scalar(msgn[:, g], mod[l][:, g], 0.0, 2.0, ALU.is_ge, ALU.mult)
                    i = nc.vector.tensor_scalar(mabs[:, g], mod[l][:, g], -1.0, 0.25, ALU.mult, ALU.max)
                i.then_inc(done, 1)
                dve.wait_ge(done, 2)
                for w in (GA, GB):
                    g = slice(w * n, w * n + n)
                    i = nc.vector.tensor_tensor(mabs[:, g], mabs[:, g], mod[l][:, g], ALU.max)
                i.then_inc(done, 1)
                dve.wait_ge(done, 3)
                for w in (GA, GB):
                    g = slice(w * n, w * n + n)
                    i = nc.vector.scalar_tensor_tensor(mod[l][:, g], msgn[:, g], -1.0, mabs[:, g], ALU.add, ALU.mult)
                i.then_inc(done, 1)
                dve.wait_ge(done, 4)
            dve.wait_ge(sg("in_x"), 16)
            dve.wait_ge(sg("in_cst"), 16)
            centre_dve(dve, "n0")
            modulation(0)
            stat_dve(dve, "n0", 1e-5)
            diag_dve(dve, "n0")
            dve.wait_ge(sg("in_lut"), 16)
            dve.wait_ge(sg("idx_pre"), 16)
            for j in range(LUT):
                nc.vector.tensor_scalar(pre_tmp[:, j * LPRE:j * LPRE + LPRE], pre_idx.bitcast(I32), float(j), lut[:, j:j + 1],
                                        ALU.is_equal, ALU.mult).then_inc(sg("pre_tmp"), 1)
            modulate_dve(dve, "n0", 0, SA, CA)
            modulation(1)
            dve.wait_ge(sg("ab_ps"), 1)
            nc.vector.tensor_copy(a_tok.rearrange("p (h i) -> p h i", i=NT),
                                  bank(0)[:, 0:NT * H].rearrange("p (i h) -> p h i", h=H)).then_inc(sg("a_sb"), 1)
            dve.wait_ge(sg("in_par"), 16)

            def turn(h, hh, par, st):
                def conv(w, s, dst):
                    dve.wait_ge(sg("a0_tap_" + s), h + 1)
                    for j in range(1, TAPS):
                        if j > 1:
                            dve.wait_ge(sg("a0_conv_" + s), 3 * h + j - 1)
                        nc.vector.scalar_tensor_tensor(by_batch(dst), by_batch(u[s])[:, :, j:j + S],
                                                       par_in[:, bass.ds(M_CW + (w * H + h) * TAPS + j, 1)],
                                                       by_batch(dst), ALU.mult, ALU.add).then_inc(sg("a0_conv_" + s), 1)

                def rope(s):
                    dve.wait_ge(sg("a0_rs_" + s), h + 1)
                    nc.vector.tensor_tensor(rot[s], rot[s], sw[s], ALU.add).then_inc(sg("a0_rope_" + s), 1)

                def look(js):
                    for j in js:
                        if j == 0 and par == 0:
                            dve.wait_ge(sg("a0_idx"), 16 * (hh + 1))
                        if j == 0 and since(h, 1):
                            dve.wait_ge(sg("a0_lut_add"), LTURN * h)
                        n = par * LTURN + j
                        nc.vector.tensor_scalar(lt[j], lidx_i, float(n), lut[:, n:n + 1], ALU.is_equal, ALU.mult)\
                            .then_inc(sg("a0_lut_tmp"), 1)

                def seams(t):
                    return t[:, T:BAND].rearrange("p (b j) -> p b j", j=PAD)

                if 2 in st:
                    dve.wait_ge(sg("a0_tanh"), h)
                    nc.vector.scalar_tensor_tensor(by_tile(gm[:, 0:T]), by_tile(gate[:, 0:T]), 1.0, over_tiles(mask, NT),
                                                   ALU.add, ALU.mult)
                    nc.vector.scalar_tensor_tensor(seams(gm), seams(gate), 1.0, over_tiles(seam, B), ALU.add, ALU.mult)\
                        .then_inc(sg("a0_gm"), 1)
                if 1 in st:
                    conv(0, "q", cq)
                    look(range(0, LTURN // 2))
                if 2 in st:
                    dve.wait_ge(sg("a0_ssqT"), h)
                    if since(h, 2):
                        dve.wait_ge(sg("a0_rqk"), h - 1)
                    nc.vector.tensor_scalar(ssq_s, bank(7)[:, P:P + 2 * NT], 1e-24, None, ALU.max).then_inc(sg("a0_ssq_s"), 1)
                if 1 in st:
                    conv(1, "k", ck)
                if 2 in st:
                    dve.wait_ge(sg("a0_S"), h)
                    dve.wait_ge(sg("a0_gm"), h)
                    if since(h, 2):
                        dve.wait_ge(sg("a0_o"), h - 1)
                    nc.vector.tensor_tensor(A, psum[:, 4 * 512:4 * 512 + BAND], gm, ALU.mult).then_inc(sg("a0_A"), 1)
                if 1 in st:
                    conv(2, "v", cv[par])
                    rope("q")
                    look(range(LTURN // 2, LTURN))
                    rope("k")
                    dve.wait_ge(sg("a0_ssq"), h + 1)
                    if since(h, 1):
                        dve.wait_ge(sg("a0_ssqT"), h)
                    nc.vector.tensor_copy(rows_sb[0:2 * NT, :], bank(7)[0:2 * NT, 0:P]).then_inc(sg("a0_rows_sb"), 1)
                if 2 in st:
                    dve.wait_ge(sg("a0_o"), h)
                    dve.wait_ge(sg("a0_silu_z"), h)
                    for n in range(NT):
                        i = (n + NT // 2) % NT
                        if n == NT // 2:
                            m.then_inc(sg("a0_g_hi"), 1)
                            dve.wait_ge(sg("a0_sqo_lo"), h)
                        c = slice(i * P, i * P + P)
                        m = nc.vector.scalar_tensor_tensor(sz[1 - par][:, c], slot(1)[:, c], rqk[1 - par][:, i:i + 1],
                                                           sz[1 - par][:, c], ALU.mult, ALU.mult)
                    m.then_inc(sg("a0_g"), 1)

            turns0(dve, turn)
            dve.wait_ge(sg("a0_sqo"), H)
            nc.vector.tensor_reduce(stat, ss_all.rearrange("p (h i) -> p i h", i=NT), AX.X, ALU.add).then_inc(sg("rms_sum"), 1)
            dve.wait_ge(sg("rms_sum"), 1)
            nc.vector.tensor_scalar(stat, stat, 1.0 / (H * HD), 1e-6, ALU.mult, ALU.add).then_inc(norm("r0", "stat")[0], 1)
            diag_dve(dve, "r0")
            dve.wait_ge(sg("idx_post"), 16)
            tail, n = lut_w[:, LUTC - LPRE:LUTC], 0
            for j in range(LUT):
                if n:
                    dve.wait_ge(sg("lut_post"), n)
                nc.vector.tensor_scalar(post_tmp if j else tail, post_idx.bitcast(I32), float(j), lut[:, j:j + 1],
                                        ALU.is_equal, ALU.mult).then_inc(sg("lut_post"), 1)
                n += 1
                if j:
                    dve.wait_ge(sg("lut_post"), n)
                    nc.vector.tensor_tensor(tail, tail, post_tmp, ALU.add).then_inc(sg("lut_post"), 1)
                    n += 1
            dve.wait_ge(sg("a0_out"), 1)
            dve.wait_ge(sg("rms_sb"), 1)
            for k in range(KC):
                i = nc.vector.tensor_tensor(chunk(ln_c, k), slot(k), rb, ALU.mult)
            i.then_inc(sg("y0"), 1)
            dve.wait_ge(sg("y0"), 1)
            residual_dve(dve, "x1", 0, GA, ln_c)
            dve.wait_ge(sg("x1"), 1)
            layer_norm_dve(dve, "n1", 0, SB_, CB)
            for m in range(MT):
                r = min(P, INTER - m * P)
                dve.wait_ge(sg("f_u"), m + 1)
                dve.wait_ge(sg("f_silu"), m + 1)
                if m >= 2:
                    dve.wait_ge(sg("f_down"), m - 1)
                nc.vector.tensor_tensor(hsb[m % 2][0:r, :], slot(1)[0:r, :], gsb[0:r, :], ALU.mult).then_inc(sg("f_h"), 1)
            dve.wait_ge(sg("f_down"), MT)
            residual_dve(dve, "x2", 0, GB, psum[:, 4 * 512:8 * 512])
            dve.wait_ge(sg("x2"), 1)
            layer_norm_dve(dve, "n2", 1, SA, CA)

            def turn1(h, hh, par, st):
                old = 1 - par

                def peak(b):
                    n = 4 * (h - 1) + b
                    m = nmax[:, 2 * b:2 * b + 2]
                    dve.wait_ge(sg("a1_S"), n + 1)
                    nc.vector.tensor_reduce(m, by_tile(bank(4 + b % 2), S), AX.X, ALU.max).then_inc(sg("a1_max"), 1)
                    dve.wait_ge(sg("a1_max"), n + 1)
                    nc.vector.tensor_scalar(m, m, -SCALE, None, ALU.mult).then_inc(sg("a1_nmax"), 1)

                def normed(b):
                    n = 4 * (h - 1) + b
                    dve.wait_ge(sg("a1_exp"), n + 1)
                    nc.vector.reciprocal(rinv[:, 2 * b:2 * b + 2], rsum[:, 2 * b:2 * b + 2]).then_inc(sg("a1_rinv"), 1)
                    dve.wait_ge(sg("a1_rinv"), n + 1)
                    for i in range(2):
                        p = prob[b % 2][:, i * S:i * S + S]
                        m = nc.vector.tensor_scalar(p, p, rinv[:, 2 * b + i:2 * b + i + 1], None, ALU.mult)
                    m.then_inc(sg("a1_norm"), 1)

                def pt_out(b):
                    dve.wait_ge(sg("a1_T"), 4 * (h - 1) + b + 1)
                    if since(h, 2):
                        dve.wait_ge(sg("a1_o"), h - 1)
                    nc.vector.tensor_copy(pt_all[:, b * 512:b * 512 + 512], bank(6 + b % 2)).then_inc(sg("a1_pt_dve"), 1)

                if 2 in st:
                    peak(0)
                    peak(1)
                    normed(0)
                    normed(1)
                    peak(2)
                    pt_out(1)
                    peak(3)
                    normed(2)
                if 1 in st:
                    dve.wait_ge(sg("a1_k"), h + 1)
                    nc.vector.tensor_scalar(k_sb[par], slot(1), par_in[:, bass.ds(M_BQKV + H + h, 1)], None, ALU.add)\
                        .then_inc(sg("a1_k_sb"), 1)
                if 2 in st:
                    normed(3)
                    pt_out(3)
                    dve.wait_ge(sg("a1_o"), h)
                    nc.vector.tensor_scalar(G[:, bass.ds((h - 1) * T, T)], slot(1), par_in[:, bass.ds(M_BQKV + 2 * H + h - 1, 1)],
                                            None, ALU.add).then_inc(sg("a1_o_sb"), 1)

            turns1(dve, turn1)
            dve.wait_ge(sg("a1_out"), 1)
            for k in range(KC):
                i = nc.vector.tensor_scalar(chunk(ln_c, k), slot(k), par_in[:, M_BO + k:M_BO + k + 1], None, ALU.add)
            i.then_inc(sg("y2"), 1)
            dve.wait_ge(sg("y2"), 1)
            residual_dve(dve, "x3", 1, GA, ln_c)
            dve.wait_ge(sg("x3"), 1)
            layer_norm_dve(dve, "n3", 1, SB_, CB)
            stat_dve(dve, "n4", 1e-6)
            diag_dve(dve, "n4")
            dve.wait_ge(*norm("n4", "spread"))
            for k in range(KC):
                i = nc.vector.scalar_tensor_tensor(chunk(xr, k), chunk(h_t, k), par_in[:, M_RMS + k:M_RMS + k + 1],
                                                   psum[:, 4 * 512:4 * 512 + T], ALU.mult, ALU.mult)
            i.then_inc(sg("xr"), 1)
            link, step = sg("moe_link"), [0]

            def done(ins):
                step[0] += 1
                ins.then_inc(link, 1)
                dve.wait_ge(link, step[0])

            v3 = {"lg": by_tile(lg, E), "ex": by_tile(ex, E), "mk": by_tile(mk, E), "eq": by_tile(eqs, E), "pos": by_tile(pos, E)}
            mx, sm = m8[:, 0:NT], m8[:, NT:2 * NT]
            dve.wait_ge(sg("moe_logits"), 1)
            done(nc.vector.tensor_reduce(mx, by_tile(bank(0, NT * E), E), AX.X, ALU.max))
            nc.vector.tensor_tensor(v3["lg"], by_tile(bank(0, NT * E), E), over_cols(mx, E), ALU.subtract)\
                .then_inc(sg("moe_shifted"), 1)
            dve.wait_ge(sg("moe_exp"), 1)
            done(nc.vector.tensor_reduce(sm, v3["ex"], AX.X, ALU.add))
            done(nc.vector.reciprocal(sm, sm))
            done(nc.vector.tensor_tensor(v3["ex"], v3["ex"], over_cols(sm, E), ALU.mult))
            for t in range(NT):
                i = nc.vector.max(m8[:, t * 8:t * 8 + 8], ex[:, t * E:t * E + E])
            done(i)
            for t in range(NT):
                i = nc.vector.max_index(mi.bitcast(U32)[:, t * 8:t * 8 + 8], m8[:, t * 8:t * 8 + 8], ex[:, t * E:t * E + E])
            done(i)
            done(nc.vector.tensor_copy(mif, mi.bitcast(U32)))
            for j in range(TOPK):
                dst = v3["mk"] if j == 0 else v3["eq"]
                done(nc.vector.tensor_tensor(dst, over_tiles(iota_e, NT), over_cols(by_tile(mif, 8)[:, :, j], E), ALU.is_equal))
                if j:
                    done(nc.vector.tensor_tensor(mk, mk, eqs, ALU.add))
            nc.vector.tensor_scalar(tot, mk, 1.0, None, ALU.mult).then_inc(sg("moe_mask"), 1)
            done(nc.vector.tensor_tensor(ex, ex, mk, ALU.mult))
            done(nc.vector.tensor_reduce(sm, v3["ex"], AX.X, ALU.add))
            done(nc.vector.reciprocal(sm, sm))
            done(nc.vector.tensor_tensor(v3["ex"], v3["ex"], over_cols(sm, E), ALU.mult))
            dve.wait_ge(sg("moe_count"), 1)
            done(nc.vector.tensor_copy(tot, bank(2, NT * E)))
            for t in range(1, NT - 1):
                done(nc.vector.tensor_tensor(tot[:, t * E:t * E + E], tot[:, t * E:t * E + E], tot[:, (t - 1) * E:t * E], ALU.add))
            nc.vector.tensor_copy(pos[:, 0:E], bank(1)[:, 0:E])
            done(nc.vector.tensor_tensor(pos[:, E:NT * E], bank(1)[:, E:NT * E], tot[:, 0:(NT - 1) * E], ALU.add))
            nc.vector.scalar_tensor_tensor(oh, pos, float(CAP - 1), mk, ALU.is_equal, ALU.mult).then_inc(sg("moe_oh"), 1)
            done(nc.vector.tensor_scalar(eqs, pos, float(CAP), -2.0, ALU.is_ge, ALU.mult))
            nc.vector.scalar_tensor_tensor(ex, eqs, 1.0, ex, ALU.add, ALU.mult).then_inc(sg("moe_code"), 1)
            dve.wait_ge(sg("star_zero"), 1)
            dve.wait_ge(sg("moe_star_ps"), 1)
            done(nc.vector.tensor_copy(t_star[:, 0:E], bank(3)[0:1, 0:E]))
            nc.vector.tensor_scalar(m8, m8, 1.0, None, ALU.mult).then_inc(sg("moe_star"), 1)

            def expert(e, par, hh):
                dve.wait_ge(sg("moe_u"), e + 1)
                dve.wait_ge(sg("moe_silu"), e + 1)
                dve.wait_ge(sg(f"moe_c{par}"), 16 * (hh + 1))
                if since(e, 2):
                    dve.wait_ge(sg("moe_down"), e - 1)
                nc.vector.tensor_tensor(aa[par], slot(1), sgl[par], ALU.mult).then_inc(sg("moe_gu"), 1)
                star = dve.value_load(t_star[0:1, bass.ds(e, 1)], min_val=0, max_val=T - 1)
                dve.wait_ge(sg("moe_gu"), e + 1)
                nc.vector.tensor_copy(a_star[:, 0:1], aa[par][:, bass.ds(star, 1)]).then_inc(sg("moe_star_sb"), 1)
                dve.wait_ge(sg("moe_star_sb"), e + 1)
                nc.vector.tensor_scalar(ov, code_b[par], 0.0, a_star[:, 0:1], ALU.min, ALU.mult)
                nc.vector.scalar_tensor_tensor(aa[par], code_b[par], 0.0, aa[par], ALU.max, ALU.mult).then_inc(sg("moe_act"), 1)
                dve.wait_ge(sg("moe_act"), 2 * e + 1)
                nc.vector.tensor_tensor(aa[par], aa[par], ov, ALU.subtract).then_inc(sg("moe_act"), 1)

            expert(0, 0, 0)
            expert(1, 1, 0)
            with dve.Fori(1, NE // 2) as i:
                expert(2 * i, 0, i)
                expert(2 * i + 1, 1, i)
            expert(NE - 1, 0, NE // 2)
            dve.wait_ge(sg("moe_down"), NE)
            nc.vector.tensor_tensor(ln_c, psum[:, 4 * 512:8 * 512], h_t, ALU.add).then_inc(sg("y3"), 1)
            dve.wait_ge(sg("y3"), 1)
            residual_dve(dve, "y_out", 1, GB, ln_c)

        @block.gpsimd
        def _(pool):
            nc.gpsimd.memset(neg_half, -0.5).then_inc(sg("half"), 1)
            nc.gpsimd.memset(small[0:1, 640:640 + NE].bitcast(I32), 0).then_inc(sg("star_zero"), 1)
            pool.wait_ge(sg("half"), 1)
            rstd_pool(pool, "n0")
            for j in range(1, LUT):
                pool.wait_ge(sg("pre_tmp"), j + 1)
                if j > 1:
                    pool.wait_ge(sg("lut_pre"), j - 1)
                nc.gpsimd.tensor_tensor(lut_w[:, 0:LPRE], pre_tmp[:, 0:LPRE] if j == 1 else lut_w[:, 0:LPRE],
                                        pre_tmp[:, j * LPRE:j * LPRE + LPRE], ALU.add).then_inc(sg("lut_pre"), 1)
            pool.wait_ge(*norm("n0", "out"))
            for s in "qkv":
                nc.gpsimd.memset(by_batch(u[s])[:, :, 0:PAD], 0.0)
            i = nc.gpsimd.memset(rows_sb, 0.0)
            i.then_inc(sg("pads"), 1)
            pool.wait_ge(sg("a_sb"), 1)
            pool.wait_ge(sg("in_cst"), 16)

            def turn(h, hh, par, st):
                def blocks(t):
                    return by_tile(t[:, 0:T])

                def seams(t):
                    return t[:, T:BAND].rearrange("p (b j) -> p b j", j=PAD)

                def add(js):
                    for j in js:
                        if j == 0 and par == 0:
                            continue
                        pool.wait_ge(sg("a0_lut_tmp"), LTURN * h + j + 1)
                        if j == 1 and par == 0:
                            if since(h, 1):
                                pool.wait_ge(sg("a0_lut_out"), 16 * hh)
                            nc.gpsimd.tensor_tensor(lacc, lt[0], lt[1], ALU.add).then_inc(sg("a0_lut_add"), 2)
                        else:
                            pool.wait_ge(sg("a0_lut_add"), LTURN * h + j)
                            nc.gpsimd.tensor_tensor(lacc, lacc, lt[j], ALU.add).then_inc(sg("a0_lut_add"), 1)

                if 2 in st:
                    pool.wait_ge(sg("a0_ssq_s"), h)
                    if since(h, 2):
                        pool.wait_ge(sg("a0_g"), h - 1)
                        pool.wait_ge(sg("a0_sqo"), h - 1)
                    nc.gpsimd.tensor_tensor(rqk[1 - par], ssq_s, neg_half, ALU.pow).then_inc(sg("a0_rqk"), 1)
                if 1 in st:
                    nc.gpsimd.tensor_copy(a_head, a_tok[:, bass.ds(h * NT, NT)]).then_inc(sg("a0_a"), 1)
                    pool.wait_ge(sg("a0_a"), h + 1)
                    pool.wait_ge(sg("a0_b"), 16 * (h + 1))
                    nc.gpsimd.tensor_tensor(seams(gate), by_batch(gate[:, 0:T])[:, :, P:P + PAD],
                                            over_cols(a_head.rearrange("p (b j) -> p b j", j=2)[:, :, 0], PAD),
                                            ALU.mult).then_inc(sg("a0_ab_seam"), 1)
                    pool.wait_ge(sg("a0_ab_seam"), h + 1)
                    nc.gpsimd.tensor_tensor(blocks(gate), blocks(gate), over_cols(a_head, P), ALU.mult).then_inc(sg("a0_ab"), 1)
                    for j, s in enumerate("qk"):
                        pool.wait_ge(sg("a0_conv_" + s), 3 * h + 3)
                        if since(h, 1):
                            pool.wait_ge(sg("a0_S"), h)
                        nc.gpsimd.tensor_tensor(by_batch(rot[s]), by_batch(c_[s]), over_tiles(cos_t, B), ALU.mult)\
                            .then_inc(sg("a0_rc_" + s), 1)
                        pool.wait_ge(sg("a0_sw_" + s), 32 * (h + 1))
                        nc.gpsimd.tensor_tensor(by_batch(sw[s]), by_batch(sw[s]), over_tiles(sin_t, B), ALU.mult)\
                            .then_inc(sg("a0_rs_" + s), 1)
                        add(range(j * LTURN // 2, (j + 1) * LTURN // 2))

            turns0(pool, turn)
            rstd_pool(pool, "r0")
            rstd_pool(pool, "n1")
            rstd_pool(pool, "n2")

            def weights(h, par, hh):
                pool.wait_ge(sg(f"a1_w{par}"), 80 * (hh + 1))
                if since(h, 2):
                    pool.wait_ge(sg("a1_v"), h - 1)
                nc.gpsimd.tensor_tensor(w1[par], code[par], scl[par], ALU.mult).then_inc(sg("a1_wmul"), 1)

            weights(0, 0, 0)
            weights(1, 1, 0)
            pool.wait_ge(sg("in_wo"), 80)
            nc.gpsimd.tensor_tensor(wo_c, wo_c, wo_s, ALU.mult).then_inc(sg("a1_womul"), 1)
            with pool.Fori(1, H // 2) as i:
                weights(2 * i, 0, i)
                weights(2 * i + 1, 1, i)
            rstd_pool(pool, "n3")
            pool.wait_ge(*norm("n3", "out"))
            nc.gpsimd.memset(code_t[E:NE, :], 1.0).then_inc(sg("code_ones"), 1)
            pool.wait_ge(sg("code_ones"), 1)
            rstd_pool(pool, "n4")


def kernel(**inputs):
    import numpy as np
    import concourse.bacc as _bacc
    from concourse.bass_utils import run_bass_kernel_spmd as _run

    x = {k: np.asarray(v) for k, v in inputs.items()}

    def rows(w):
        return np.ascontiguousarray(w.reshape(-1, P, w.shape[1]).transpose(1, 0, 2)).reshape(P, -1)

    def heads(ws):
        return np.ascontiguousarray(np.stack([w.reshape(KC, P, H, HD) for w in ws]).transpose(3, 2, 0, 1, 4)).reshape(H, P, -1)

    def per_head(v):
        return v.reshape(H, P).T

    f = np.float32
    d_, s_ = np.arange(P), np.arange(S)
    inv = (1.0 / f(1000000.0) ** (np.arange(0, HD, 2, dtype=f) / f(HD))).astype(f)
    ang = (s_.astype(f)[None, :] * inv[:, None]).astype(f)
    lag = d_[None, :] - d_[:, None]
    seam_lag = P + np.arange(PAD)[None, :] - d_[:, None]
    cst = np.concatenate([
        np.eye(P), np.ones((P, P)), np.full((P, P), 1.0 / D), lag > 0,
        ((lag >= 0) & (lag < TAPS)) * (0.5 * SCALE), (seam_lag < TAPS) * (0.5 * SCALE),
        np.cos(np.concatenate([ang, ang])), np.concatenate([-np.sin(ang), np.sin(ang)]),
        np.tile(np.arange(E), (P, 1)), d_[:, None] + P * np.arange(NT)[None, :],
        np.tile(np.arange(4 * NT - 1) == 2 * NT - 1, (P, 1))], axis=1).astype(f)
    idx = np.zeros((P, LUTC), np.int32)
    idx[:, 0:UPC] = rows(x["L0_ffn_gate_idx"].T)
    idx[:, UPC:2 * UPC] = rows(x["L0_ffn_up_idx"].T)
    down = np.zeros((MT * P, D), np.int32)
    down[0:INTER] = x["L0_ffn_down_idx"].T
    idx[:, 2 * UPC:] = rows(down)
    qkv_scales = np.stack([x[f"L1_attn_w{j}_scales"].reshape(KC, 4, H, HD) for j in "qkv"])
    moe = np.zeros((NE, P, EW), f)
    moe[0:E, :, 0:2 * D] = x["L1_ffn_w13"].reshape(E, KC, P, D).transpose(0, 2, 1, 3).reshape(E, P, 2 * D)
    moe[0:E, :, 2 * D:] = x["L1_ffn_w2"]
    moe[E, :, 0:2 * D] = rows(np.concatenate([x["L1_ffn_shared_gate_w"], x["L1_ffn_shared_up_w"]], axis=1))
    moe[E, :, 2 * D:] = x["L1_ffn_shared_down_w"]
    arrays = {
        "x": rows(x["L0_attn_x"].reshape(T, D).T),
        "c0": rows(x["L0_c"].T), "c1": rows(x["L1_c"].T),
        "wmod0": rows(x["L0_wmod"]), "wmod1": rows(x["L1_wmod"]),
        "cst": cst,
        "par_in": np.concatenate(
            [x[f"L0_attn_conv_{j}_w"].reshape(H, P, TAPS).transpose(1, 0, 2).reshape(P, -1) for j in "qkv"]
            + [per_head(x["L0_attn_norm_w"]), rows(x["L0_attn_Wa"]), rows(x["L0_attn_Wb"])]
            + [per_head(x[f"L1_attn_b{j}"]) for j in "qkv"]
            + [x["L1_attn_bo"].reshape(KC, P).T, x["L1_ffn_norm_w"].reshape(KC, P).T, rows(x["L1_ffn_gate_w"].T)], axis=1),
        "lut": x["L0_ffn_lut"].reshape(1, LUT),
        "idx_pre": idx[:, 0:LPRE], "idx_post": idx[:, LUTC - LPRE:],
        "idx": idx[:, LPRE:LUTC - LPRE].reshape(P, H // 2, LW).transpose(1, 0, 2),
        "w_qkvz": heads([x[f"L0_attn_W{j}"] for j in "qkvz"]),
        "w_out": rows(x["L0_attn_Wout"]),
        "qkv_codes": heads([x[f"L1_attn_w{j}_codes"] for j in "qkv"]),
        "qkv_scales": np.ascontiguousarray(qkv_scales.transpose(3, 2, 0, 1, 4)).reshape(H, 4, QKV),
        "wo_codes": rows(x["L1_attn_wo_codes"]),
        "wo_scales": np.ascontiguousarray(x["L1_attn_wo_scales"].reshape(H, 4, D).transpose(1, 0, 2)).reshape(4, H * D),
        "w_moe": moe,
    }
    nc = _bacc.Bacc("TRN2", target_bir_lowering=False, num_devices=1)
    arrays = {k: np.ascontiguousarray(v) for k, v in arrays.items()}
    aps = {k: nc.dram_tensor("in_" + k, v.shape, mybir.dt.from_np(v.dtype), kind="ExternalInput").ap() for k, v in arrays.items()}
    out = nc.dram_tensor("out_0", (P, KC * T), F32, kind="ExternalOutput").ap()
    b_rows = nc.dram_tensor("b_rows", (H, T), F32, kind="Internal").ap()
    code_rows = nc.dram_tensor("code_rows", (NE, T), F32, kind="Internal").ap()
    build(nc, aps, out, b_rows, code_rows)
    r = _run(nc, [{"in_" + k: v for k, v in arrays.items()}], core_ids=[0])
    y = r.results[0]["out_0"]
    return np.ascontiguousarray(y.reshape(P, KC, B, S).transpose(2, 3, 1, 0)).reshape(B, S, D)
```

```python
from contextlib import ExitStack

import concourse.bass as bass
from concourse import mybir

ALU = mybir.AluOpType
ACT = mybir.ActivationFunctionType
AX = mybir.AxisListType
F32 = mybir.dt.float32
F32R = mybir.dt.float32r
I32 = mybir.dt.int32
U32 = mybir.dt.uint32

P = 128
B, S, D = 4, 256, 256
T = B * S
KC = D // P
NT = T // P
H, HD, TAPS = 16, 128, 4
PAD = TAPS - 1
BAND = T + B * PAD
INTER, LUT = 688, 16
MT = -(-INTER // P)
UPC = KC * INTER
LUTC = 2 * UPC + MT * D
LW = LUTC // H
LTURN = LUT // 2
LPRE, LPOST = 2 * LW, 6 * LW
E, TOPK, CAP = 32, 4, 256
NE = E + 1
QKV = 3 * KC * P
EW = 3 * D
SCALE = float(HD) ** -0.5
assert LW * H == LUTC and HD == P

C_ID, C_ONE, C_INV, C_STRICT, C_MASK, C_SEAM, C_COS, C_SIN, C_IOTA, C_TOK = 0, 128, 256, 384, 512, 640, 643, 899, 1155, 1187
C_SEL = 1195
C_ALL = C_SEL + 4 * NT - 1
M_CW, M_NW, M_WBA, M_BQKV, M_BO, M_RMS, M_GW = 0, 192, 208, 272, 320, 322, 324
M_ALL = 324 + KC * E

def build(nc, a, out, b_rows, code_rows):
    ctx = ExitStack()
    named = {}

    def sg(name):
        if name not in named:
            named[name] = ctx.enter_context(nc.semaphore(name))
        return named[name]

    def norm(tag, step, k=KC - 1):
        order = [t for t in ("n0", "r0", "n1", "n2", "n3", "n4")
                 if t not in {"mean": "r0 n4", "centred": "r0 n4", "scaled": "r0 n4", "out": "r0 n4", "sq": "r0", "var": "r0", "rows": "r0", "rows_sb": "r0"}
                 .get(step, "").split()]
        if step in ("centred", "sq", "scaled", "out"):
            return sg("norm_" + step), order.index(tag) * KC + k + 1
        return sg("norm_" + step), order.index(tag) + 1

    def sb(name, cols, dt=F32):
        return ctx.enter_context(nc.sbuf_tensor(name, [P, cols], dt))[:, :]

    def twice(name, cols):
        with nc.sbuf_tensor(name, [P, cols], F32) as t:
            plain = t[:, :]
        return plain, sb(name + "_r", cols, F32R)

    with ctx:
        psum = ctx.enter_context(nc.psum_tensor("psum", [P, 8 * 512], F32))[:, :]

        def bank(i, n=512):
            return psum[:, i * 512:i * 512 + n]

        x_t, h_t = sb("x_t", KC * T), sb("h_t", KC * T)
        cst, par_in = sb("cst", C_ALL), sb("par_in", M_ALL)
        lut_w, lut_w_r = twice("lut_w", LUTC)
        ident, ones, inv_d = cst[:, C_ID:C_ID + P], cst[:, C_ONE:C_ONE + P], cst[:, C_INV:C_INV + P]
        strict, mask, seam = cst[:, C_STRICT:C_STRICT + P], cst[:, C_MASK:C_MASK + P], cst[:, C_SEAM:C_SEAM + PAD]
        cos_t, sin_t = cst[:, C_COS:C_COS + S], cst[:, C_SIN:C_SIN + S]
        iota_e, tok_id = cst[:, C_IOTA:C_IOTA + E], cst[:, C_TOK:C_TOK + NT]
        small = sb("small", 680)
        used = [0]

        def few(n):
            v = small[:, used[0]:used[0] + n]
            used[0] += n
            assert used[0] <= 640
            return v

        mod = [few(6 * KC * B), few(6 * KC * B)]
        msgn, mabs = few(6 * KC * B), few(6 * KC * B)
        stat, rstd, neg_half = few(NT), few(NT), few(2 * NT)
        ct = [few(KC * B), few(KC * B)]
        a_tok, a_head = few(H * NT), few(NT)
        ssq_s, rqk0, rqk1 = few(2 * NT), few(2 * NT), few(2 * NT)
        rqk = [rqk0, rqk1]
        ss_all = few(H * NT)
        nmax, rsum, rinv = few(8), few(8), few(8)
        lut = few(LUT)
        a_star = few(2)
        ARENA = 25408
        arena, arena_r = twice("arena", ARENA)
        G, halves = twice("G", H * T)

        def carve(*sizes, base=0, of=arena):
            o, v = base, []
            for n in sizes:
                v.append(of[:, o:o + n])
                o += n
            assert o <= ARENA, o
            return v

        UW = B * (S + PAD)
        (uq, uk, uv, cq, ck, cv0, cv1, swq, swk, qr, kr, sqq, sqk, sz0, sz1, gate, gm, A, v_tok, junk,
         wh0, wh1, lidx, lt_all, lacc, rows_sb) = carve(
            UW, UW, UW, T, T, T, T, T, T, T, T, T, T, T, T, BAND, BAND, BAND, T, T,
            4 * KC * P, 4 * KC * P, LW, LTURN * LW, LW, P)
        u, c_ = {"q": uq, "k": uk, "v": uv}, {"q": cq, "k": ck}
        sw, rot, sqr = {"q": swq, "k": swk}, {"q": qr, "k": kr}, {"q": sqq, "k": sqk}
        cv, sz, wh = [cv0, cv1], [sz0, sz1], [wh0, wh1]
        lt = [lt_all[:, j * LW:j * LW + LW] for j in range(LTURN)]
        lidx_i = lidx.bitcast(I32)
        wmod = [G[:, 0:KC * 6 * D], G[:, KC * 6 * D:2 * KC * 6 * D]]
        ba_sb = G[0:2 * H, 2 * KC * 6 * D:2 * KC * 6 * D + T]

        (pre_idx, pre_tmp) = carve(LPRE, LUT * LPRE, base=5 * T)
        ln_c, ln_sq, ln_b, rb, gsb, hsb0, hsb1, post_idx, post_tmp = carve(KC * T, KC * T, T, T, T, T, T, LPOST, 4 * LPOST)
        post = [post_tmp[:, j * LPOST:j * LPOST + LPOST] for j in range(4)]
        (wout,) = carve(H * D, base=ARENA - P - (LTURN + 2) * LW - 8 * KC * P)
        hsb = [hsb0, hsb1]
        QK = 2 * KC * P
        (qh0, qh1, ql0, ql1, k_h, k_l, vh0, vh1, vl0, vl1) = carve(*[T] * 10, of=arena_r)
        p0, p1 = carve(512, 512, base=10 * T)
        pt_h, pt_l = carve(4 * 512, 4 * 512, base=11 * T, of=arena_r)
        code, scl, w10, w11 = carve(QKV, QKV, QKV, QKV, base=15 * T)
        wqh0, wqh1, wql0, wql1 = carve(QK, QK, QK, QK, base=15 * T + 4 * QKV, of=arena_r)
        (wo_c,) = carve(H * D, base=15 * T + 4 * QKV + 4 * QK)
        (wo_s,) = carve(H * D, base=9 * T)
        hh_h, hh_l = lut_w_r[:, 0:KC * T], lut_w_r[:, KC * T:2 * KC * T]
        q_h, q_l, v_h, v_l = [qh0, qh1], [ql0, ql1], [vh0, vh1], [vl0, vl1]
        prob, w1, w1_h, w1_l = [p0, p1], [w10, w11], [wqh0, wqh1], [wql0, wql1]
        (xr, we0, we1, cb0, cb1, sg0, sg1, aa0, aa1, ov, code_t, oh, lg, ex, mk, eqs, pos, tot, m8, mi, mif) = carve(
            KC * T, EW, EW, T, T, T, T, T, T, T, T, NT * E, NT * E, NT * E, NT * E, NT * E, NT * E, NT * E,
            NT * 8, NT * 8, NT * 8, base=5 * T)
        we, code_b, sgl, aa = [we0, we1], [cb0, cb1], [sg0, sg1], [aa0, aa1]
        xr_h, xr_l = halves[:, 0:KC * T], halves[:, KC * T:2 * KC * T]
        aa_h = [halves[:, (2 * KC + i) * T:(2 * KC + i + 1) * T] for i in range(2)]
        aa_l = [halves[:, (2 * KC + 2 + i) * T:(2 * KC + 3 + i) * T] for i in range(2)]
        eh = [halves[:, (2 * KC + 4) * T + i * EW:(2 * KC + 4) * T + i * EW + EW] for i in range(2)]
        el = [halves[:, (2 * KC + 4) * T + (2 + i) * EW:(2 * KC + 4) * T + (3 + i) * EW] for i in range(2)]
        t_star = small[0:1, 640:640 + NE].bitcast(I32)

        def chunk(t, k):
            return t[:, k * T:(k + 1) * T]

        def by_batch(v):
            return v.rearrange("p (b s) -> p b s", b=B)

        def by_tile(v, n=P):
            return v.rearrange("p (i t) -> p i t", t=n)

        def over_cols(v, n):
            return v.unsqueeze(2).broadcast_to([P, v.shape[1], n])

        def over_tiles(v, n):
            return v.unsqueeze(1).broadcast_to([P, n, v.shape[1]])

        def modv(l, w, k, b):
            c = (w * KC + k) * B + b
            return mod[l][:, c:c + 1]

        SA, CA, GA, SB_, CB, GB = range(6)

        block = ctx.enter_context(nc.Block())

        def mean_pe(pe, tag, changed=None):
            for k in range(KC):
                if changed is not None:
                    pe.wait_ge(sg("x_new"), KC * changed + k + 1)
                for n in range(2):
                    i = nc.tensor.matmul(bank(n), inv_d, x_t[:, k * T + n * 512:k * T + n * 512 + 512],
                                         start=(k == 0), stop=(k == KC - 1))
            i.then_inc(norm(tag, "mean")[0], 1)

        def select(i):
            return cst[:, C_SEL + 2 * NT - 1 - i:C_SEL + 4 * NT - 1 - i]

        def var_pe(pe, tag):
            for k in range(KC):
                pe.wait_ge(*norm(tag, "sq", k))
                for t in range(NT):
                    i = nc.tensor.matmul(bank(2)[0:2 * NT, 0:P], select(t), ln_sq[:, k * T + t * P:k * T + t * P + P],
                                         start=(t == 0 and k == 0), stop=(t == NT - 1 and k == KC - 1))
            i.then_inc(norm(tag, "rows")[0], 1)
            pe.wait_ge(*norm(tag, "rows_sb"))
            nc.tensor.transpose(bank(3)[:, 0:2 * NT], ln_b[0:2 * NT, 0:P], ident[0:2 * NT, 0:2 * NT])\
                .then_inc(norm(tag, "var")[0], 1)

        def spread_pe(pe, tag):
            pe.wait_ge(*norm(tag, "diag"))
            for n in range(2):
                i = nc.tensor.matmul(bank(4 + n), ones, ln_b[:, n * 512:n * 512 + 512], start=True, stop=True)
            i.then_inc(norm(tag, "spread")[0], 1)

        def square_act(act, tag, src, ready):
            for k in range(KC):
                act.wait_ge(*norm(*ready, k))
                nc.scalar.activation(chunk(ln_sq, k), chunk(src, k), ACT.Square).then_inc(norm(tag, "sq")[0], 1)

        def centre_dve(dve, tag):
            dve.wait_ge(*norm(tag, "mean"))
            for k in range(KC):
                nc.vector.tensor_tensor(chunk(ln_c, k), chunk(x_t, k), psum[:, 0:T], ALU.subtract)\
                    .then_inc(norm(tag, "centred")[0], 1)

        def stat_dve(dve, tag, eps):
            dve.wait_ge(*norm(tag, "rows"))
            nc.vector.tensor_copy(ln_b[0:2 * NT, 0:P], bank(2)[0:2 * NT, 0:P]).then_inc(norm(tag, "rows_sb")[0], 1)
            dve.wait_ge(*norm(tag, "var"))
            nc.vector.tensor_scalar(stat, bank(3)[:, 0:NT], 1.0 / D, eps, ALU.mult, ALU.add).then_inc(norm(tag, "stat")[0], 1)

        def diag_dve(dve, tag):
            dve.wait_ge(*norm(tag, "rstd"))
            nc.vector.tensor_tensor(by_tile(ln_b), over_tiles(ident, NT), over_cols(rstd, P), ALU.mult)\
                .then_inc(norm(tag, "diag")[0], 1)

        def rstd_pool(pool, tag):
            pool.wait_ge(*norm(tag, "stat"))
            nc.gpsimd.tensor_tensor(rstd, stat, neg_half[:, 0:NT], ALU.pow).then_inc(norm(tag, "rstd")[0], 1)

        def modulate_dve(dve, tag, l, w_shift, w_scale):
            dve.wait_ge(*norm(tag, "spread"))
            for k in range(KC):
                nc.vector.tensor_tensor(chunk(ln_c, k), chunk(ln_c, k), psum[:, 4 * 512:4 * 512 + T], ALU.mult)\
                    .then_inc(norm(tag, "scaled")[0], 1)
            for k in range(KC):
                dve.wait_ge(*norm(tag, "scaled", k))
                for b in range(B):
                    c = slice(k * T + b * S, k * T + b * S + S)
                    i = nc.vector.tensor_scalar(h_t[:, c], ln_c[:, c], modv(l, w_scale, k, b), modv(l, w_shift, k, b),
                                                ALU.mult, ALU.add)
                i.then_inc(norm(tag, "out")[0], 1)

        def layer_norm_dve(dve, tag, l, w_shift, w_scale):
            centre_dve(dve, tag)
            stat_dve(dve, tag, 1e-5)
            diag_dve(dve, tag)
            modulate_dve(dve, tag, l, w_shift, w_scale)

        def layer_norm_pe(pe, tag, changed):
            mean_pe(pe, tag, changed)
            var_pe(pe, tag)
            spread_pe(pe, tag)

        def residual_dve(dve, done, l, w, y, k):
            for b in range(B):
                c = slice(k * T + b * S, k * T + b * S + S)
                i = nc.vector.scalar_tensor_tensor(x_t[:, c], y[:, c], modv(l, w, k, b), x_t[:, c], ALU.mult, ALU.add)
            i.then_inc(sg(done), 1)

        def post_sum(eng, ops, j, done, c):
            tail = lut_w[:, LUTC - LPOST:LUTC][:, c]
            if j > 1:
                eng.wait_ge(sg(done), j - 1)
            ops.tensor_tensor(tail, post[0][:, c] if j == 1 else tail, post[j % 4][:, c], ALU.add).then_inc(sg(done), 1)

        def slot(i):
            return psum[:, i * T:i * T + T]

        def s_block(i):
            return psum[:, 4 * 512 + i * P:4 * 512 + i * P + P]

        def s_seam(b):
            return psum[:, 4 * 512 + T + b * PAD:4 * 512 + T + b * PAD + PAD]

        def turns0(eng, turn):
            turn(0, 0, 0, (1,))
            turn(1, 0, 1, (1, 2))
            with eng.Fori(1, H // 2) as i:
                turn(2 * i, i, 0, (1, 2, 3))
                turn(2 * i + 1, i, 1, (1, 2, 3))
            turn(H, H // 2, 0, (2, 3))
            turn(H + 1, H // 2, 1, (3,))

        def turns1(eng, turn):
            turn(0, 0, 0, (1,))
            turn(1, 0, 1, (1, 2))
            with eng.Fori(1, H // 2) as i:
                turn(2 * i, i, 0, (1, 2))
                turn(2 * i + 1, i, 1, (1, 2))
            turn(H, H // 2, 0, (2,))

        def since(h, n):
            return not isinstance(h, int) or h >= n

        def evens(h):
            return min(h + 1, H) if isinstance(h, int) else h + 1

        @block.sync
        def _(sp):
            sp.dma_start(ct[0], a["c0"]).then_inc(sg("in_c"), 16)
            sp.dma_start(ct[1], a["c1"]).then_inc(sg("in_c"), 16)
            sp.dma_start(x_t, a["x"]).then_inc(sg("in_x"), 16)
            sp.dma_start(cst, a["cst"]).then_inc(sg("in_cst"), 16)
            sp.dma_start(wmod[0], a["wmod0"]).then_inc(sg("in_wmod0"), 16)
            sp.dma_start(wmod[1], a["wmod1"]).then_inc(sg("in_wmod1"), 16)
            sp.dma_start(par_in, a["par_in"]).then_inc(sg("in_par"), 16)
            sp.dma_start(lut, a["lut"].broadcast_to([P, LUT])).then_inc(sg("in_lut"), 16)
            sp.dma_start(pre_idx.bitcast(I32), a["idx_pre"]).then_inc(sg("in_idx"), 16)
            sp.dma_start(lidx_i, a["idx"][0]).then_inc(sg("a0_idx"), 16)
            for par in range(2):
                sp.dma_start(wh[par], a["w_qkvz"][par]).then_inc(sg(f"a0_w{par}"), 16)
            sp.wait_ge(sg("ba_sb"), 1)
            sp.dma_start(b_rows, ba_sb[0:H, :]).then_inc(sg("b_rows"), 16)
            sp.wait_ge(sg("b_rows"), 16)

            def lut_out(h, hh):
                sp.wait_ge(sg("a0_lut_add"), LTURN * (h + 1))
                sp.dma_start(lut_w[:, bass.ds(LPRE + hh * LW, LW)], lacc).then_inc(sg("a0_lut_out"), 16)

            def turn(h, hh, par, ahead):
                if since(h, 1):
                    sp.wait_ge(sg("a0_gm"), h)
                sp.dma_start(gate[:, 0:T], b_rows[bass.ds(h, 1), :].broadcast_to([P, T])).then_inc(sg("a0_b"), 16)
                for s in "qk":
                    if since(h, 1):
                        sp.wait_ge(sg("a0_rope_" + s), h)
                    sp.wait_ge(sg("a0_conv_" + s), 3 * h + 3)
                    sp.dma_start(sw[s][0:64, :], c_[s][64:128, :]).then_inc(sg("a0_sw_" + s), 16)
                    sp.dma_start(sw[s][64:128, :], c_[s][0:64, :]).then_inc(sg("a0_sw_" + s), 16)
                if ahead:
                    sp.wait_ge(sg("a0_z"), h + 1)
                    sp.dma_start(wh[par], a["w_qkvz"][h + 2]).then_inc(sg(f"a0_w{par}"), 16)
                if par == 1:
                    lut_out(h, hh)
                    if ahead:
                        sp.wait_ge(sg("a0_lut_tmp"), LTURN * (h + 1))
                        sp.dma_start(lidx_i, a["idx"][hh + 1]).then_inc(sg("a0_idx"), 16)

            turn(0, 0, 0, True)
            turn(1, 0, 1, True)
            with sp.Fori(1, H // 2 - 1) as i:
                turn(2 * i, i, 0, True)
                turn(2 * i + 1, i, 1, True)
            turn(H - 2, H // 2 - 1, 0, False)
            turn(H - 1, H // 2 - 1, 1, False)
            sp.wait_ge(sg("a0_z"), H)
            sp.wait_ge(sg("a0_lut_out"), 16 * (H // 2))
            sp.dma_start(wout, a["w_out"]).then_inc(sg("in_wout"), 16)
            sp.wait_ge(sg("a0_gT_sb"), H)
            sp.dma_start(post_idx.bitcast(I32), a["idx_post"]).then_inc(sg("in_idx"), 16)

            sp.wait_ge(sg("lut_post_dve"), LUT - 1)
            sp.wait_ge(sg("lut_post_pool"), LUT - 1)
            sp.wait_ge(sg("attn_out"), KC)

            def load1(h):
                sp.dma_start(code, a["qkv_codes"][h]).then_inc(sg("a1_code"), 16)
                for g in range(4):
                    sp.dma_start(scl[32 * g:32 * g + 32, :], a["qkv_scales"][h][g:g + 1, :].broadcast_to([32, QKV]))\
                        .then_inc(sg("a1_code"), 16)

            load1(0)
            sp.dma_start(wo_c, a["wo_codes"]).then_inc(sg("in_wo"), 16)
            for g in range(4):
                sp.dma_start(wo_s[32 * g:32 * g + 32, :], a["wo_scales"][g:g + 1, :].broadcast_to([32, H * D]))\
                    .then_inc(sg("in_wo"), 16)
            with sp.Fori(1, H) as h:
                sp.wait_ge(sg("a1_wmul"), h)
                load1(h)

            def load_up(e, par):
                sp.dma_start(we[par][:, 0:2 * D], a["w_moe"][e][:, 0:2 * D]).then_inc(sg(f"moe_w13_{par}"), 16)

            def load_down(e, par):
                sp.dma_start(we[par][:, 2 * D:EW], a["w_moe"][e][:, 2 * D:EW]).then_inc(sg(f"moe_w2_{par}"), 16)

            def load_code(e, par):
                sp.dma_start(code_b[par], code_rows[bass.ds(e, 1), :].broadcast_to([P, T])).then_inc(sg(f"moe_c{par}"), 16)

            sp.wait_ge(sg("a1_o"), H)
            for e in range(2):
                load_up(e, e)
                load_down(e, e)
            sp.wait_ge(sg("moe_codeT"), 1)
            sp.dma_start(code_rows, code_t[0:NE, :]).then_inc(sg("code_rows"), 16)

            sp.wait_ge(sg("code_rows"), 16)
            for e in range(2):
                load_code(e, e)
            for e in range(2):
                sp.wait_ge(sg("moe_w13_lo"), e + 1)
                load_up(e + 2, e)

            def load_e(e, par, ahead=True):
                sp.wait_ge(sg("moe_act"), 2 * (e - 1))
                load_code(e, par)
                sp.wait_ge(sg("moe_w2_lo"), e - 1)
                load_down(e, par)
                if ahead:
                    sp.wait_ge(sg("moe_w13_lo"), e + 1)
                    load_up(e + 2, par)

            with sp.Fori(1, NE // 2 - 1) as i:
                load_e(2 * i, 0)
                load_e(2 * i + 1, 1)
            load_e(NE - 3, 0)
            load_e(NE - 2, 1, ahead=False)
            load_e(NE - 1, 0, ahead=False)
            for k in range(KC):
                sp.wait_ge(sg("y_out"), k + 1)
                sp.dma_start(out[:, k * T:(k + 1) * T], chunk(x_t, k)).then_inc(sg("out_written"), 16)
            sp.wait_ge(sg("out_written"), 16 * KC)

        @block.tensor
        def _(pe):
            def modulation(l):
                pe.wait_ge(sg("silu_c"), 2)
                pe.wait_ge(sg(f"in_wmod{l}"), 16)
                for f in range(6 * KC):
                    for k in range(KC):
                        i = nc.tensor.matmul(bank(6 + l)[:, f * B:f * B + B],
                                             wmod[l][:, k * 6 * D + f * P:k * 6 * D + f * P + P],
                                             ct[l][:, k * B:k * B + B], start=(k == 0), stop=(k == KC - 1))
                i.then_inc(sg("mod_ps"), 1)

            pe.wait_ge(sg("in_x"), 16)
            pe.wait_ge(sg("in_cst"), 16)
            mean_pe(pe, "n0")
            modulation(0)
            var_pe(pe, "n0")
            spread_pe(pe, "n0")
            modulation(1)

            def by_halves(dst, w_h, w_l, x_h, x_l, start, stop):
                nc.tensor.matmul(dst, w_l, x_h, start=start, stop=False, skip_group_check=True)
                nc.tensor.matmul(dst, w_h, x_l, start=False, stop=False, skip_group_check=True)
                return nc.tensor.matmul(dst, w_h, x_h, start=False, stop=stop, skip_group_check=True)

            pe.wait_ge(*norm("n0", "out"))
            pe.wait_ge(sg("in_par"), 16)
            for n in range(2):
                for k in range(KC):
                    i = nc.tensor.matmul(bank(4 + n)[0:2 * H, :], par_in[:, M_WBA + k * 2 * H:M_WBA + (k + 1) * 2 * H],
                                         h_t[:, k * T + n * 512:k * T + n * 512 + 512], start=(k == 0), stop=(k == KC - 1))
            i.then_inc(sg("ba_ps"), 1)
            pe.wait_ge(sg("ba_sb"), 1)
            for t in range(NT):
                i = nc.tensor.transpose(bank(6)[:, t * 2 * H:t * 2 * H + 2 * H], ba_sb[:, t * P:t * P + P],
                                        ident[0:2 * H, 0:2 * H])
            i.then_inc(sg("ba_ps"), 1)

            def project(dst, w, rows, n_w=KC):
                for n in range(2):
                    for k in range(n_w):
                        i = nc.tensor.matmul(dst[0:rows, n * 512:n * 512 + 512], w(k),
                                             h_t[:, k * T + n * 512:k * T + n * 512 + 512],
                                             start=(k == 0), stop=(k == n_w - 1))
                return i

            def turn(h, hh, par, st):
                def w(j, k):
                    return wh[par][:, (j * KC + k) * P:(j * KC + k) * P + P]

                if 1 in st:
                    pe.wait_ge(sg(f"a0_w{par}"), 16 * (hh + 1))
                    if since(h, 1):
                        pe.wait_ge(sg("a0_silu_v"), h)
                    if since(h, 2):
                        pe.wait_ge(sg("a0_v_tok"), h - 1)
                    project(slot(0), lambda k: w(0, k), P).then_inc(sg("a0_q"), 1)
                if 2 in st:
                    pe.wait_ge(sg("a0_rows_sb"), h)
                    if since(h, 2):
                        pe.wait_ge(sg("a0_ssq_s"), h - 1)
                    nc.tensor.transpose(bank(7)[:, P:2 * P], rows_sb, ident)\
                        .then_inc(sg("a0_ssqT"), 1)
                if 3 in st:
                    pe.wait_ge(sg("a0_g"), h - 1)
                    pe.wait_ge(sg("a0_A"), h - 1)
                    for i in range(NT):
                        t = nc.tensor.transpose(s_block(i), sz[par][:, i * P:i * P + P], ident)
                    t.then_inc(sg("a0_gT"), 1)
                if 1 in st:
                    if since(h, 1):
                        pe.wait_ge(sg("a0_silu_z"), h)
                    if since(h, 2):
                        pe.wait_ge(sg("a0_g"), h - 1)
                        pe.wait_ge(sg("a0_sqo"), h - 1)
                    project(slot(1), lambda k: w(1, k), P).then_inc(sg("a0_k"), 1)
                    pe.wait_ge(sg("a0_silu_q"), h + 1)
                    project(slot(0), lambda k: w(2, k), P).then_inc(sg("a0_v"), 1)
                if 2 in st:
                    pe.wait_ge(sg("a0_rope_q"), h)
                    pe.wait_ge(sg("a0_rope_k"), h)
                    if since(h, 2):
                        pe.wait_ge(sg("a0_gT_sb"), h - 1)
                        pe.wait_ge(sg("a0_A"), h - 1)
                    for i in range(NT):
                        nc.tensor.matmul(s_block(i), kr[:, i * P:i * P + P], qr[:, i * P:i * P + P], start=True, stop=True)
                    for b in range(B):
                        i = nc.tensor.matmul(s_seam(b), kr[:, b * S:b * S + P], qr[:, b * S + P:b * S + P + PAD],
                                             start=True, stop=True)
                    i.then_inc(sg("a0_S"), 1)
                if 1 in st:
                    pe.wait_ge(sg("a0_silu_k"), h + 1)
                    for t in range(NT):
                        for k in range(KC):
                            i = nc.tensor.matmul(slot(1)[:, t * P:t * P + P], h_t[:, k * T + t * P:k * T + t * P + P],
                                                 w(3, k), start=(k == 0), stop=(k == KC - 1))
                    i.then_inc(sg("a0_z"), 1)
                if 2 in st:
                    pe.wait_ge(sg("a0_conv_v"), 3 * h)
                    pe.wait_ge(sg("a0_silu_v"), evens(h))
                    for i in range(NT):
                        t = nc.tensor.transpose(slot(0)[:, i * P:i * P + P], cv[1 - par][:, i * P:i * P + P], ident)
                    t.then_inc(sg("a0_vT"), 1)
                if 1 in st:
                    for j, s in enumerate("qk"):
                        pe.wait_ge(sg("a0_sq_" + s), h + 1)
                        if since(h, 1) and j == 0:
                            pe.wait_ge(sg("a0_ssq_s"), h)
                        for i in range(NT):
                            n = j * NT + i
                            m = nc.tensor.matmul(bank(7)[0:2 * NT, 0:P], select(n), sqr[s][:, i * P:i * P + P],
                                                 start=(n == 0), stop=(n == 2 * NT - 1))
                    m.then_inc(sg("a0_ssq"), 1)
                if 2 in st:
                    pe.wait_ge(sg("a0_A"), h)
                    pe.wait_ge(sg("a0_v_tok"), h)
                    pe.wait_ge(sg("a0_silu_z"), evens(h))
                    for i in range(NT):
                        o = slot(1)[:, i * P:i * P + P]
                        m = nc.tensor.matmul(o, A[:, i * P:i * P + P], v_tok[:, i * P:i * P + P], start=True, stop=(i % 2 == 0),
                                             skip_group_check=True)
                        if i % 2:
                            c = T + (i // 2) * PAD
                            m = nc.tensor.matmul(o[0:PAD, :], A[:, c:c + PAD], v_tok[:, (i - 1) * P:i * P], start=False,
                                                 stop=True, skip_group_check=True)
                    m.then_inc(sg("a0_o"), 1)

            turns0(pe, turn)
            pe.wait_ge(sg("in_wout"), 16)
            pe.wait_ge(sg("a0_gT_sb"), H)
            pe.wait_ge(sg("a0_sqo"), H)

            def out_project(w, between=lambda: None):
                for m in range(KC):
                    for n in range(2):
                        for h in range(H):
                            i = nc.tensor.matmul(bank(2 * m + n), w[:, h * D + m * P:h * D + m * P + P],
                                                 G[:, h * T + n * 512:h * T + n * 512 + 512], start=(h == 0), stop=(h == H - 1))
                    i.then_inc(sg("attn_out"), 1)
                    if m == 0:
                        between()

            out_project(wout, lambda: spread_pe(pe, "r0"))

            layer_norm_pe(pe, "n1", 0)
            pe.wait_ge(*norm("n1", "out"))
            pe.wait_ge(sg("lut_pre"), LUT - 1)
            pe.wait_ge(sg("a0_lut_out"), 16 * (H // 2))
            pe.wait_ge(sg("lut_post_dve"), LUT - 1)
            pe.wait_ge(sg("lut_post_pool"), LUT - 1)
            def down(m):
                r = min(P, INTER - m * P)
                pe.wait_ge(sg("f_h"), m + 1)
                for o in range(KC):
                    for n in range(2):
                        i = nc.tensor.matmul(bank(4 + 2 * o + n), lut_w[0:r, 2 * UPC + m * D + o * P:2 * UPC + m * D + o * P + P],
                                             hsb[m % 2][0:r, n * 512:n * 512 + 512], start=(m == 0), stop=(m == MT - 1))
                    i.then_inc(sg("f_down"), 1)

            for m in range(MT):
                r = min(P, INTER - m * P)
                if m:
                    pe.wait_ge(sg("f_silu"), m)
                project(slot(0), lambda k: lut_w[:, k * INTER + m * P:k * INTER + m * P + r], r).then_inc(sg("f_g"), 1)
                if m:
                    pe.wait_ge(sg("f_h"), m)
                project(slot(1), lambda k: lut_w[:, UPC + k * INTER + m * P:UPC + k * INTER + m * P + r], r)\
                    .then_inc(sg("f_u"), 1)
                if m:
                    down(m - 1)
            down(MT - 1)

            layer_norm_pe(pe, "n2", 1)
            pe.wait_ge(*norm("n2", "out"))

            def project_by_halves(dst, par, j):
                for n in range(2):
                    for k in range(KC):
                        w, c = slice((j * KC + k) * P, (j * KC + k) * P + P), slice(k * T + n * 512, k * T + n * 512 + 512)
                        i = by_halves(dst[:, n * 512:n * 512 + 512], w1_h[par][:, w], w1_l[par][:, w], hh_h[:, c], hh_l[:, c],
                                      k == 0, k == KC - 1)
                return i

            def turn1(h, hh, par, st):
                old = 1 - par

                def w(j, k):
                    return w1[par][:, (j * KC + k) * P:(j * KC + k) * P + P]

                def scores(b):
                    if b < 2:
                        if since(h, 2):
                            pe.wait_ge(sg("a1_exp"), 4 * (h - 2) + b + 3)
                    else:
                        pe.wait_ge(sg("a1_exp"), 4 * (h - 1) + b - 1)
                    for i in range(2):
                        c = slice(b * S + i * P, b * S + i * P + P)
                        m = by_halves(bank(4 + b % 2)[:, i * S:i * S + S], q_h[old][:, c], q_l[old][:, c],
                                      k_h[:, b * S:b * S + S], k_l[:, b * S:b * S + S], True, True)
                    m.then_inc(sg("a1_S"), 1)

                def turned(b):
                    pe.wait_ge(sg("a1_norm"), 4 * (h - 1) + b + 1)
                    if b >= 2 or since(h, 2):
                        pe.wait_ge(sg("a1_pt_lo"), 4 * (h - 1) + b - 1)
                    for i in range(2):
                        for j in range(2):
                            t = nc.tensor.transpose(bank(6 + b % 2)[:, j * S + i * P:j * S + i * P + P],
                                                    prob[b % 2][:, i * S + j * P:i * S + j * P + P], ident)
                    t.then_inc(sg("a1_T"), 1)

                if 2 in st:
                    pe.wait_ge(sg("a1_lo"), 3 * h - 1)
                    scores(0)
                    scores(1)
                if 1 in st:
                    pe.wait_ge(sg("a1_w_lo"), h + 1)
                    if since(h, 1):
                        pe.wait_ge(sg("a1_lo"), 3 * h)
                    project_by_halves(slot(0), par, 0).then_inc(sg("a1_q"), 1)
                if 2 in st:
                    turned(0)
                    scores(2)
                    turned(1)
                    scores(3)
                if 1 in st:
                    if since(h, 2):
                        pe.wait_ge(sg("a1_o_sb"), h - 1)
                    elif h == 1:
                        pe.wait_ge(sg("a1_lo"), 2)
                    project_by_halves(slot(1), par, 1).then_inc(sg("a1_k"), 1)
                def v_tiles(ts):
                    for t in ts:
                        for k in range(KC):
                            i = nc.tensor.matmul(slot(0)[:, t * P:t * P + P], h_t[:, k * T + t * P:k * T + t * P + P],
                                                 w(2, k), start=(k == 0), stop=(k == KC - 1))
                    return i

                if 1 in st:
                    pe.wait_ge(sg("a1_lo"), 3 * h + 1)
                    v_tiles(range(0, 3))
                if 2 in st:
                    turned(2)
                    turned(3)
                if 1 in st:
                    v_tiles(range(3, NT)).then_inc(sg("a1_v"), 1)
                if 2 in st:
                    pe.wait_ge(sg("a1_lo"), 3 * h + 2 if 1 in st else 3 * h)
                    pe.wait_ge(sg("a1_pt_lo"), 4 * h)
                    for b in range(B):
                        for j in range(2):
                            c, t = slice((2 * b + j) * P, (2 * b + j + 1) * P), slice(b * 512 + j * S, b * 512 + j * S + S)
                            m = by_halves(slot(1)[:, b * S:b * S + S], v_h[old][:, c], v_l[old][:, c], pt_h[:, t], pt_l[:, t],
                                          j == 0, j == 1)
                    m.then_inc(sg("a1_o"), 1)

            pe.wait_ge(sg("in_lo"), KC)
            turns1(pe, turn1)
            pe.wait_ge(sg("a1_womul"), 1)
            pe.wait_ge(sg("a1_o_sb"), H)
            out_project(wo_c)

            layer_norm_pe(pe, "n3", 2)
            var_pe(pe, "n4")
            spread_pe(pe, "n4")
            pe.wait_ge(sg("xr"), 1)
            for t in range(NT):
                for k in range(KC):
                    i = nc.tensor.matmul(bank(4)[:, t * E:t * E + E], xr[:, k * T + t * P:k * T + t * P + P],
                                         par_in[:, M_GW + k * E:M_GW + k * E + E], start=(k == 0), stop=(k == KC - 1))
            i.then_inc(sg("moe_logits"), 1)
            pe.wait_ge(sg("in_hi"), KC + 1)
            pe.wait_ge(sg("in_lo"), KC + 1)

            def up_e(e, par):
                pe.wait_ge(sg("moe_w13_hi"), e + 1)
                pe.wait_ge(sg("moe_w13_lo"), e + 1)
                for j, (ready, done) in enumerate((("moe_silu", "moe_g"), ("moe_gu", "moe_u"))):
                    if since(e, 1):
                        pe.wait_ge(sg(ready), e)
                    for n in range(2):
                        for k in range(KC):
                            w, c = slice(k * D + j * P, k * D + j * P + P), slice(k * T + n * 512, k * T + n * 512 + 512)
                            i = by_halves(slot(j)[:, n * 512:n * 512 + 512], eh[par][:, w], el[par][:, w], xr_h[:, c], xr_l[:, c],
                                          k == 0, k == KC - 1)
                    i.then_inc(sg(done), 1)

            up_e(0, 0)
            pe.wait_ge(sg("moe_mask"), 1)
            nc.tensor.matmul(bank(5)[:, 0:NT * E], strict, mk, start=True, stop=True)
            nc.tensor.matmul(bank(6)[:, 0:NT * E], ones, mk, start=True, stop=True).then_inc(sg("moe_count"), 1)
            pe.wait_ge(sg("moe_oh"), 1)
            for t in range(NT):
                i = nc.tensor.matmul(bank(7)[0:1, 0:E], tok_id[:, t:t + 1], oh[:, t * E:t * E + E], start=(t == 0), stop=(t == NT - 1))
            i.then_inc(sg("moe_star_ps"), 1)
            pe.wait_ge(sg("moe_code"), 1)
            for t in range(NT):
                i = nc.tensor.transpose(psum[0:E, 4 * 512 + t * P:4 * 512 + t * P + P],
                                        ex[:, t * E:t * E + E], ident)
            i.then_inc(sg("moe_codeT_ps"), 1)
            def down_e(e, par, first=False, last=False):
                pe.wait_ge(sg("moe_w2_hi"), e + 1)
                pe.wait_ge(sg("moe_w2_lo"), e + 1)
                pe.wait_ge(sg("moe_hi"), e + 1)
                pe.wait_ge(sg("moe_lo"), e + 1)
                for m in range(KC):
                    for n in range(2):
                        w, c = slice(2 * D + m * P, 2 * D + m * P + P), slice(n * 512, n * 512 + 512)
                        i = by_halves(bank(4 + 2 * m + n), eh[par][:, w], el[par][:, w], aa_h[par][:, c], aa_l[par][:, c],
                                      first, last)
                    if last or m == KC - 1:
                        i.then_inc(sg("moe_down"), 1)

            up_e(1, 1)
            up_e(2, 0)
            pe.wait_ge(sg("moe_codeT"), 1)
            pe.wait_ge(sg("moe_star"), 1)
            down_e(0, 0, first=True)
            up_e(3, 1)
            down_e(1, 1)
            with pe.Fori(2, NE // 2) as i:
                up_e(2 * i, 0)
                down_e(2 * i - 2, 0)
                up_e(2 * i + 1, 1)
                down_e(2 * i - 1, 1)
            up_e(NE - 1, 0)
            down_e(NE - 3, 0)
            down_e(NE - 2, 1)
            down_e(NE - 1, 0, last=True)

        @block.scalar
        def _(act):
            act.wait_ge(sg("in_c"), 32)
            for l in range(2):
                nc.scalar.activation(ct[l], ct[l], ACT.Silu).then_inc(sg("silu_c"), 1)
            square_act(act, "n0", ln_c, ("n0", "centred"))
            act.wait_ge(sg("ba_ps"), 1)
            nc.scalar.activation(ba_sb, psum[0:2 * H, 4 * 512:4 * 512 + T], ACT.Copy).then_inc(sg("ba_sb"), 1)

            def turn(h, hh, par, st):
                def cw(w, j):
                    return par_in[:, bass.ds(M_CW + (w * H + h) * TAPS + j, 1)]

                def silu_and_tap(w, s, dst):
                    act.wait_ge(sg("a0_" + s), h + 1)
                    if since(h, 1):
                        act.wait_ge(sg("a0_conv_" + s), 3 * h)
                    nc.scalar.activation(by_batch(u[s])[:, :, PAD:PAD + S], by_batch(slot({"q": 0, "k": 1, "v": 0}[s])),
                                         ACT.Silu).then_inc(sg("a0_silu_" + s), 1)
                    act.wait_ge(sg("a0_silu_" + s), h + 1)
                    if s == "v":
                        if since(h, 2):
                            act.wait_ge(sg("a0_vT"), h - 1)
                    elif since(h, 1):
                        act.wait_ge(sg("a0_sw_" + s), 32 * h)
                        act.wait_ge(sg("a0_rc_" + s), h)
                        act.wait_ge(sg("a0_sq_" + s), h)
                    nc.scalar.activation(by_batch(dst), by_batch(u[s])[:, :, 0:S], ACT.Copy, scale=cw(w, 0))\
                        .then_inc(sg("a0_tap_" + s), 1)

                if 1 in st:
                    if not since(h, 1):
                        act.wait_ge(sg("pool_set"), 3)
                        act.wait_ge(sg("in_par"), 16)
                    silu_and_tap(0, "q", cq)
                if 3 in st:
                    act.wait_ge(sg("a0_gT"), h - 1)
                    nc.scalar.activation(G[:, bass.ds((h - 2) * T, T)], psum[:, 4 * 512:4 * 512 + T], ACT.Copy,
                                         scale=par_in[:, bass.ds(M_NW + h - 2, 1)]).then_inc(sg("a0_gT_sb"), 1)
                if 1 in st:
                    silu_and_tap(1, "k", ck)
                    silu_and_tap(2, "v", cv[par])
                    for s in "qk":
                        act.wait_ge(sg("a0_conv_" + s), 3 * h + 3)
                        if since(h, 1):
                            act.wait_ge(sg("a0_ssq"), h)
                        nc.scalar.activation(sqr[s], c_[s], ACT.Square).then_inc(sg("a0_sq_" + s), 1)
                    act.wait_ge(sg("a0_z"), h + 1)
                    if since(h, 2):
                        act.wait_ge(sg("a0_gT"), h - 1)
                    nc.scalar.activation(sz[par], slot(1), ACT.Silu).then_inc(sg("a0_silu_z"), 1)
                    act.wait_ge(sg("a0_ab"), h + 1)
                    nc.scalar.activation(gate, gate, ACT.Tanh, scale=0.5).then_inc(sg("a0_tanh"), 1)
                if 2 in st:
                    act.wait_ge(sg("a0_vT"), h)
                    if since(h, 2):
                        act.wait_ge(sg("a0_o"), h - 1)
                    act.wait_ge(sg("a0_rqk"), h)
                    for i in range(NT):
                        c = slice(i * P, i * P + P)
                        m = nc.scalar.activation(v_tok[:, c], slot(0)[:, c], ACT.Copy,
                                                 scale=rqk[1 - par][:, NT + i:NT + i + 1])
                    m.then_inc(sg("a0_v_tok"), 1)
                    act.wait_ge(sg("a0_o"), h)
                    if since(h, 2):
                        act.wait_ge(sg("a0_sqo"), h - 1)
                    for i in range(NT):
                        if i == NT // 2:
                            m.then_inc(sg("a0_sqo_lo"), 1)
                            act.wait_ge(sg("a0_g_hi"), h)
                        m = nc.scalar.activation(junk[:, i * P:i * P + P], slot(1)[:, i * P:i * P + P], ACT.Square, scale=rqk[1 - par][:, i:i + 1],
                                                 accum_out=ss_all[:, bass.ds((h - 1) * NT + i, 1)])
                    m.then_inc(sg("a0_sqo"), 1)

            turns0(act, turn)
            act.wait_ge(*norm("r0", "spread"))
            nc.scalar.activation(rb, psum[:, 4 * 512:4 * 512 + T], ACT.Copy).then_inc(sg("rms_sb"), 1)
            square_act(act, "n1", ln_c, ("n1", "centred"))
            for m in range(MT):
                r = min(P, INTER - m * P)
                act.wait_ge(sg("f_g"), m + 1)
                if m:
                    act.wait_ge(sg("f_h"), m)
                nc.scalar.activation(gsb[0:r, :], slot(0)[0:r, :], ACT.Silu).then_inc(sg("f_silu"), 1)
            square_act(act, "n2", ln_c, ("n2", "centred"))

            def turn1(h, hh, par, st):
                old = 1 - par

                def expo(b):
                    n = 4 * (h - 1) + b
                    act.wait_ge(sg("a1_nmax"), n + 1)
                    if b >= 2:
                        act.wait_ge(sg("a1_T"), n - 1)
                    elif since(h, 2):
                        act.wait_ge(sg("a1_T"), n - 1)
                    for i in range(2):
                        e = nc.scalar.activation(prob[b % 2][:, i * S:i * S + S], bank(4 + b % 2)[:, i * S:i * S + S], ACT.Exp,
                                                 bias=nmax[:, 2 * b + i:2 * b + i + 1], scale=SCALE,
                                                 accum_out=rsum[:, 2 * b + i:2 * b + i + 1])
                    e.then_inc(sg("a1_exp"), 1)

                def pt_upper(b):
                    act.wait_ge(sg("a1_T"), 4 * (h - 1) + b + 1)
                    nc.scalar.activation(pt_h[:, b * 512:b * 512 + 512], bank(6 + b % 2), ACT.Copy).then_inc(sg("a1_pt_hi"), 1)

                if 1 in st:
                    act.wait_ge(sg("a1_wmul"), h + 1)
                    nc.scalar.activation(w1_h[par], w1[par][:, 0:QK], ACT.Copy).then_inc(sg("a1_w_hi"), 1)
                if 2 in st:
                    expo(0)
                    expo(1)
                if 1 in st:
                    act.wait_ge(sg("a1_q"), h + 1)
                    nc.scalar.activation(q_h[par], slot(0), ACT.Identity, bias=par_in[:, bass.ds(M_BQKV + h, 1)])\
                        .then_inc(sg("a1_hi"), 1)
                if 2 in st:
                    pt_upper(0)
                    expo(2)
                    pt_upper(1)
                    expo(3)
                if 1 in st:
                    act.wait_ge(sg("a1_k"), h + 1)
                    nc.scalar.activation(k_h, slot(1), ACT.Identity, bias=par_in[:, bass.ds(M_BQKV + H + h, 1)])\
                        .then_inc(sg("a1_hi"), 1)
                if 2 in st:
                    pt_upper(2)
                    pt_upper(3)
                if 1 in st:
                    act.wait_ge(sg("a1_v"), h + 1)
                    nc.scalar.activation(v_h[par], slot(0), ACT.Copy).then_inc(sg("a1_hi"), 1)

            for k in range(KC):
                act.wait_ge(*norm("n2", "out", k))
                nc.scalar.activation(chunk(hh_h, k), chunk(h_t, k), ACT.Copy).then_inc(sg("in_hi"), 1)
            turns1(act, turn1)
            square_act(act, "n3", ln_c, ("n3", "centred"))
            square_act(act, "n4", h_t, ("n3", "out"))
            def upper_13(e, par, hh):
                act.wait_ge(sg(f"moe_w13_{par}"), 16 * (hh + 1))
                if since(e, 2):
                    act.wait_ge(sg("moe_u"), e - 1)
                nc.scalar.activation(eh[par][:, 0:2 * D], we[par][:, 0:2 * D], ACT.Copy).then_inc(sg("moe_w13_hi"), 1)

            act.wait_ge(sg("attn_out"), 2 * KC)
            upper_13(0, 0, 0)
            upper_13(1, 1, 0)
            act.wait_ge(sg("xr"), 1)
            nc.scalar.activation(xr_h, xr, ACT.Copy).then_inc(sg("in_hi"), 1)
            act.wait_ge(sg("moe_shifted"), 1)
            nc.scalar.activation(ex, lg, ACT.Exp).then_inc(sg("moe_exp"), 1)
            act.wait_ge(sg("moe_codeT_ps"), 1)
            act.wait_ge(sg("pool_set"), 4)
            nc.scalar.activation(code_t[0:E, :], psum[0:E, 4 * 512:4 * 512 + T], ACT.Copy).then_inc(sg("moe_codeT"), 1)

            def expert(e, par, hh, ahead=True):
                act.wait_ge(sg("moe_g"), e + 1)
                if since(e, 2):
                    act.wait_ge(sg("moe_gu"), e - 1)
                nc.scalar.activation(sgl[par], slot(0), ACT.Silu).then_inc(sg("moe_silu"), 1)
                act.wait_ge(sg(f"moe_w2_{par}"), 16 * (hh + 1))
                if since(e, 2):
                    act.wait_ge(sg("moe_down"), e - 1)
                nc.scalar.activation(eh[par][:, 2 * D:EW], we[par][:, 2 * D:EW], ACT.Copy).then_inc(sg("moe_w2_hi"), 1)
                act.wait_ge(sg("moe_act"), 2 * (e + 1))
                nc.scalar.activation(aa_h[par], aa[par], ACT.Copy).then_inc(sg("moe_hi"), 1)
                if ahead:
                    upper_13(e + 2, par, hh + 1)

            expert(0, 0, 0)
            expert(1, 1, 0)
            with act.Fori(1, NE // 2 - 1) as i:
                expert(2 * i, 0, i)
                expert(2 * i + 1, 1, i)
            expert(NE - 3, 0, NE // 2 - 1)
            expert(NE - 2, 1, NE // 2 - 1, ahead=False)
            expert(NE - 1, 0, NE // 2, ahead=False)

        @block.vector
        def _(dve):
            def modulation(l):
                dve.wait_ge(sg("mod_ps"), l + 1)
                n = KC * B
                done = sg("mod")
                nc.vector.tensor_copy(mod[l], bank(6 + l)[:, 0:6 * n]).then_inc(done, 1)
                dve.wait_ge(done, 4 * l + 1)
                for w in (CA, CB):
                    nc.vector.tensor_scalar(mod[l][:, w * n:w * n + n], mod[l][:, w * n:w * n + n], 1.0, None, ALU.add)
                for w in (GA, GB):
                    g = slice(w * n, w * n + n)
                    nc.vector.tensor_scalar(msgn[:, g], mod[l][:, g], 0.0, 2.0, ALU.is_ge, ALU.mult)
                    i = nc.vector.tensor_scalar(mabs[:, g], mod[l][:, g], -1.0, 0.25, ALU.mult, ALU.max)
                i.then_inc(done, 1)
                dve.wait_ge(done, 4 * l + 2)
                for w in (GA, GB):
                    g = slice(w * n, w * n + n)
                    i = nc.vector.tensor_tensor(mabs[:, g], mabs[:, g], mod[l][:, g], ALU.max)
                i.then_inc(done, 1)
                dve.wait_ge(done, 4 * l + 3)
                for w in (GA, GB):
                    g = slice(w * n, w * n + n)
                    i = nc.vector.scalar_tensor_tensor(mod[l][:, g], msgn[:, g], -1.0, mabs[:, g], ALU.add, ALU.mult)
                i.then_inc(done, 1)
                dve.wait_ge(done, 4 * l + 4)
            dve.wait_ge(sg("in_x"), 16)
            dve.wait_ge(sg("in_cst"), 16)
            centre_dve(dve, "n0")
            modulation(0)
            stat_dve(dve, "n0", 1e-5)
            diag_dve(dve, "n0")
            dve.wait_ge(sg("in_lut"), 16)
            dve.wait_ge(sg("in_idx"), 16)
            for j in range(LUT):
                nc.vector.tensor_scalar(pre_tmp[:, j * LPRE:j * LPRE + LPRE], pre_idx.bitcast(I32), float(j), lut[:, j:j + 1],
                                        ALU.is_equal, ALU.mult).then_inc(sg("lut_tmp"), 1)
            modulate_dve(dve, "n0", 0, SA, CA)
            modulation(1)
            dve.wait_ge(sg("ba_ps"), 2)
            nc.vector.tensor_copy(a_tok.rearrange("p (h i) -> p h i", i=NT),
                                  bank(6)[:, 0:NT * 2 * H].rearrange("p (i c) -> p c i", c=2 * H)[:, H:2 * H, :])\
                .then_inc(sg("a_sb"), 1)
            dve.wait_ge(sg("in_par"), 16)

            def turn(h, hh, par, st):
                def conv(w, s, dst):
                    dve.wait_ge(sg("a0_tap_" + s), h + 1)
                    for j in range(1, TAPS):
                        if j > 1:
                            dve.wait_ge(sg("a0_conv_" + s), 3 * h + j - 1)
                        nc.vector.scalar_tensor_tensor(by_batch(dst), by_batch(u[s])[:, :, j:j + S],
                                                       par_in[:, bass.ds(M_CW + (w * H + h) * TAPS + j, 1)],
                                                       by_batch(dst), ALU.mult, ALU.add).then_inc(sg("a0_conv_" + s), 1)

                def rope(s):
                    dve.wait_ge(sg("a0_rs_" + s), h + 1)
                    nc.vector.tensor_tensor(rot[s], rot[s], sw[s], ALU.add).then_inc(sg("a0_rope_" + s), 1)

                def look(js):
                    for j in js:
                        if j == 0 and par == 0:
                            dve.wait_ge(sg("a0_idx"), 16 * (hh + 1))
                        if j == 0 and since(h, 1):
                            dve.wait_ge(sg("a0_lut_add"), LTURN * h)
                        n = par * LTURN + j
                        nc.vector.tensor_scalar(lt[j], lidx_i, float(n), lut[:, n:n + 1], ALU.is_equal, ALU.mult)\
                            .then_inc(sg("a0_lut_tmp"), 1)

                def seams(t):
                    return t[:, T:BAND].rearrange("p (b j) -> p b j", j=PAD)

                if 2 in st:
                    dve.wait_ge(sg("a0_tanh"), h)
                    nc.vector.scalar_tensor_tensor(by_tile(gm[:, 0:T]), by_tile(gate[:, 0:T]), 1.0, over_tiles(mask, NT),
                                                   ALU.add, ALU.mult)
                    nc.vector.scalar_tensor_tensor(seams(gm), seams(gate), 1.0, over_tiles(seam, B), ALU.add, ALU.mult)\
                        .then_inc(sg("a0_gm"), 1)
                if 1 in st:
                    conv(0, "q", cq)
                if 2 in st:
                    dve.wait_ge(sg("a0_ssqT"), h)
                    if since(h, 2):
                        dve.wait_ge(sg("a0_rqk"), h - 1)
                    nc.vector.tensor_scalar(ssq_s, bank(7)[:, P:P + 2 * NT], 1e-24, None, ALU.max).then_inc(sg("a0_ssq_s"), 1)
                if 1 in st:
                    look(range(0, LTURN // 2))
                    conv(1, "k", ck)
                if 2 in st:
                    dve.wait_ge(sg("a0_S"), h)
                    dve.wait_ge(sg("a0_gm"), h)
                    if since(h, 2):
                        dve.wait_ge(sg("a0_o"), h - 1)
                    nc.vector.tensor_tensor(A, psum[:, 4 * 512:4 * 512 + BAND], gm, ALU.mult).then_inc(sg("a0_A"), 1)
                if 1 in st:
                    conv(2, "v", cv[par])
                    rope("q")
                    look(range(LTURN // 2, LTURN))
                    dve.wait_ge(sg("a0_ssq"), h + 1)
                    if since(h, 1):
                        dve.wait_ge(sg("a0_ssqT"), h)
                    nc.vector.tensor_copy(rows_sb[0:2 * NT, :], bank(7)[0:2 * NT, 0:P]).then_inc(sg("a0_rows_sb"), 1)
                if 2 in st:
                    dve.wait_ge(sg("a0_o"), h)
                    dve.wait_ge(sg("a0_silu_z"), h)
                    for n in range(NT):
                        i = (n + NT // 2) % NT
                        if n == NT // 2:
                            m.then_inc(sg("a0_g_hi"), 1)
                            dve.wait_ge(sg("a0_sqo_lo"), h)
                        c = slice(i * P, i * P + P)
                        m = nc.vector.scalar_tensor_tensor(sz[1 - par][:, c], slot(1)[:, c], rqk[1 - par][:, i:i + 1],
                                                           sz[1 - par][:, c], ALU.mult, ALU.mult)
                    m.then_inc(sg("a0_g"), 1)
                if 1 in st:
                    rope("k")

            turns0(dve, turn)
            dve.wait_ge(sg("a0_sqo"), H)
            nc.vector.tensor_reduce(stat, ss_all.rearrange("p (h i) -> p i h", i=NT), AX.X, ALU.add).then_inc(sg("rms_sum"), 1)
            dve.wait_ge(sg("rms_sum"), 1)
            nc.vector.tensor_scalar(stat, stat, 1.0 / (H * HD), 1e-6, ALU.mult, ALU.add).then_inc(norm("r0", "stat")[0], 1)
            diag_dve(dve, "r0")
            dve.wait_ge(sg("in_idx"), 32)
            for j in range(LUT):
                if j >= len(post):
                    dve.wait_ge(sg("lut_post_pool"), max(1, j - len(post)))
                nc.vector.tensor_scalar(post[j % 4], post_idx.bitcast(I32), float(j), lut[:, j:j + 1],
                                        ALU.is_equal, ALU.mult).then_inc(sg("lut_tmp"), 1)
                if j:
                    dve.wait_ge(sg("lut_tmp"), LUT + j + 1)
                    post_sum(dve, nc.vector, j, "lut_post_dve", slice(0, LPOST // 2))
            for k in range(KC):
                dve.wait_ge(sg("attn_out"), k + 1)
                if k == 0:
                    dve.wait_ge(sg("rms_sb"), 1)
                nc.vector.tensor_tensor(chunk(ln_c, k), slot(k), rb, ALU.mult).then_inc(sg("y"), 1)
                dve.wait_ge(sg("y"), k + 1)
                residual_dve(dve, "x_new", 0, GA, ln_c, k)
            dve.wait_ge(sg("x_new"), KC)
            layer_norm_dve(dve, "n1", 0, SB_, CB)
            for m in range(MT):
                r = min(P, INTER - m * P)
                dve.wait_ge(sg("f_u"), m + 1)
                dve.wait_ge(sg("f_silu"), m + 1)
                if m >= 2:
                    dve.wait_ge(sg("f_down"), KC * (m - 1))
                nc.vector.tensor_tensor(hsb[m % 2][0:r, :], slot(1)[0:r, :], gsb[0:r, :], ALU.mult).then_inc(sg("f_h"), 1)
            for k in range(KC):
                dve.wait_ge(sg("f_down"), KC * (MT - 1) + k + 1)
                residual_dve(dve, "x_new", 0, GB, psum[:, 4 * 512:8 * 512], k)
            dve.wait_ge(sg("x_new"), 2 * KC)
            layer_norm_dve(dve, "n2", 1, SA, CA)
            for k in range(KC):
                dve.wait_ge(sg("in_hi"), k + 1)
                nc.vector.tensor_tensor(chunk(hh_l, k), chunk(h_t, k), chunk(hh_h, k).bitcast(F32), ALU.subtract)\
                    .then_inc(sg("in_lo"), 1)

            def turn1(h, hh, par, st):
                old = 1 - par

                def peak(b):
                    n = 4 * (h - 1) + b
                    m = nmax[:, 2 * b:2 * b + 2]
                    dve.wait_ge(sg("a1_S"), n + 1)
                    nc.vector.tensor_reduce(m, by_tile(bank(4 + b % 2), S), AX.X, ALU.max).then_inc(sg("a1_max"), 1)
                    dve.wait_ge(sg("a1_max"), n + 1)
                    nc.vector.tensor_scalar(m, m, -SCALE, None, ALU.mult).then_inc(sg("a1_nmax"), 1)

                def normed(b):
                    n = 4 * (h - 1) + b
                    dve.wait_ge(sg("a1_exp"), n + 1)
                    nc.vector.reciprocal(rinv[:, 2 * b:2 * b + 2], rsum[:, 2 * b:2 * b + 2]).then_inc(sg("a1_rinv"), 1)
                    dve.wait_ge(sg("a1_rinv"), n + 1)
                    for i in range(2):
                        p = prob[b % 2][:, i * S:i * S + S]
                        m = nc.vector.tensor_scalar(p, p, rinv[:, 2 * b + i:2 * b + i + 1], None, ALU.mult)
                    m.then_inc(sg("a1_norm"), 1)

                def lower(n, dst, src, upper, bias=None):
                    dve.wait_ge(sg("a1_hi"), 3 * h + n)
                    if bias is None:
                        m = nc.vector.tensor_tensor(dst, src, upper.bitcast(F32), ALU.subtract)
                    else:
                        m = nc.vector.scalar_tensor_tensor(dst, src, par_in[:, bass.ds(M_BQKV + bias, 1)], upper.bitcast(F32),
                                                           ALU.add, ALU.subtract)
                    m.then_inc(sg("a1_lo"), 1)

                def pt_lower(b):
                    c = slice(b * 512, b * 512 + 512)
                    dve.wait_ge(sg("a1_pt_hi"), 4 * (h - 1) + b + 1)
                    nc.vector.tensor_tensor(pt_l[:, c], bank(6 + b % 2), pt_h[:, c].bitcast(F32), ALU.subtract)\
                        .then_inc(sg("a1_pt_lo"), 1)

                if 2 in st:
                    peak(0)
                    peak(1)
                    normed(0)
                    normed(1)
                if 1 in st:
                    lower(1, q_l[par], slot(0), q_h[par], h)
                if 2 in st:
                    peak(2)
                    pt_lower(0)
                    peak(3)
                    normed(2)
                    pt_lower(1)
                    normed(3)
                if 1 in st:
                    lower(2, k_l, slot(1), k_h, H + h)
                if 2 in st:
                    pt_lower(2)
                    pt_lower(3)
                if 1 in st:
                    lower(3, v_l[par], slot(0), v_h[par])
                if 2 in st:
                    dve.wait_ge(sg("a1_o"), h)
                    nc.vector.tensor_scalar(G[:, bass.ds((h - 1) * T, T)], slot(1), par_in[:, bass.ds(M_BQKV + 2 * H + h - 1, 1)],
                                            None, ALU.add).then_inc(sg("a1_o_sb"), 1)

            turns1(dve, turn1)
            for k in range(KC):
                dve.wait_ge(sg("attn_out"), KC + k + 1)
                nc.vector.tensor_scalar(chunk(ln_c, k), slot(k), par_in[:, M_BO + k:M_BO + k + 1], None, ALU.add)\
                    .then_inc(sg("y"), 1)
                dve.wait_ge(sg("y"), KC + k + 1)
                residual_dve(dve, "x_new", 1, GA, ln_c, k)
            dve.wait_ge(sg("x_new"), 3 * KC)
            layer_norm_dve(dve, "n3", 1, SB_, CB)
            stat_dve(dve, "n4", 1e-6)
            diag_dve(dve, "n4")
            dve.wait_ge(*norm("n4", "spread"))
            for k in range(KC):
                i = nc.vector.scalar_tensor_tensor(chunk(xr, k), chunk(h_t, k), par_in[:, M_RMS + k:M_RMS + k + 1],
                                                   psum[:, 4 * 512:4 * 512 + T], ALU.mult, ALU.mult)
            i.then_inc(sg("xr"), 1)
            link, step = sg("moe_link"), [0]

            def done(ins):
                step[0] += 1
                ins.then_inc(link, 1)
                dve.wait_ge(link, step[0])

            v3 = {"lg": by_tile(lg, E), "ex": by_tile(ex, E), "mk": by_tile(mk, E), "eq": by_tile(eqs, E), "pos": by_tile(pos, E)}
            mx, sm = m8[:, 0:NT], m8[:, NT:2 * NT]
            dve.wait_ge(sg("moe_logits"), 1)
            done(nc.vector.tensor_reduce(mx, by_tile(bank(4, NT * E), E), AX.X, ALU.max))
            nc.vector.tensor_tensor(v3["lg"], by_tile(bank(4, NT * E), E), over_cols(mx, E), ALU.subtract)\
                .then_inc(sg("moe_shifted"), 1)
            dve.wait_ge(sg("moe_exp"), 1)
            done(nc.vector.tensor_reduce(sm, v3["ex"], AX.X, ALU.add))
            done(nc.vector.reciprocal(sm, sm))
            done(nc.vector.tensor_tensor(v3["ex"], v3["ex"], over_cols(sm, E), ALU.mult))
            for t in range(NT):
                i = nc.vector.max(m8[:, t * 8:t * 8 + 8], ex[:, t * E:t * E + E])
            done(i)
            for t in range(NT):
                i = nc.vector.max_index(mi.bitcast(U32)[:, t * 8:t * 8 + 8], m8[:, t * 8:t * 8 + 8], ex[:, t * E:t * E + E])
            done(i)
            done(nc.vector.tensor_copy(mif, mi.bitcast(U32)))
            for j in range(TOPK):
                dst = v3["mk"] if j == 0 else v3["eq"]
                done(nc.vector.tensor_tensor(dst, over_tiles(iota_e, NT), over_cols(by_tile(mif, 8)[:, :, j], E), ALU.is_equal))
                if j:
                    done(nc.vector.tensor_tensor(mk, mk, eqs, ALU.add))
            nc.vector.tensor_scalar(tot, mk, 1.0, None, ALU.mult).then_inc(sg("moe_mask"), 1)
            done(nc.vector.tensor_tensor(ex, ex, mk, ALU.mult))
            done(nc.vector.tensor_reduce(sm, v3["ex"], AX.X, ALU.add))
            done(nc.vector.reciprocal(sm, sm))
            done(nc.vector.tensor_tensor(v3["ex"], v3["ex"], over_cols(sm, E), ALU.mult))
            dve.wait_ge(sg("moe_count"), 1)
            done(nc.vector.tensor_copy(tot, bank(6, NT * E)))
            for t in range(1, NT - 1):
                done(nc.vector.tensor_tensor(tot[:, t * E:t * E + E], tot[:, t * E:t * E + E], tot[:, (t - 1) * E:t * E], ALU.add))
            nc.vector.tensor_copy(pos[:, 0:E], bank(5)[:, 0:E])
            done(nc.vector.tensor_tensor(pos[:, E:NT * E], bank(5)[:, E:NT * E], tot[:, 0:(NT - 1) * E], ALU.add))
            nc.vector.scalar_tensor_tensor(oh, pos, float(CAP - 1), mk, ALU.is_equal, ALU.mult).then_inc(sg("moe_oh"), 1)
            done(nc.vector.tensor_scalar(eqs, pos, float(CAP), -2.0, ALU.is_ge, ALU.mult))
            nc.vector.scalar_tensor_tensor(ex, eqs, 1.0, ex, ALU.add, ALU.mult).then_inc(sg("moe_code"), 1)
            dve.wait_ge(sg("pool_set"), 2)
            dve.wait_ge(sg("moe_star_ps"), 1)
            done(nc.vector.tensor_copy(t_star[:, 0:E], bank(7)[0:1, 0:E]))
            nc.vector.tensor_scalar(m8, m8, 1.0, None, ALU.mult).then_inc(sg("moe_star"), 1)

            def expert(e, par, hh):
                dve.wait_ge(sg("moe_u"), e + 1)
                dve.wait_ge(sg("moe_silu"), e + 1)
                dve.wait_ge(sg(f"moe_c{par}"), 16 * (hh + 1))
                if since(e, 2):
                    dve.wait_ge(sg("moe_lo"), e - 1)
                nc.vector.tensor_tensor(aa[par], slot(1), sgl[par], ALU.mult).then_inc(sg("moe_gu"), 1)
                star = dve.value_load(t_star[0:1, bass.ds(e, 1)], min_val=0, max_val=T - 1)
                dve.wait_ge(sg("moe_gu"), e + 1)
                nc.vector.tensor_copy(a_star[:, 0:1], aa[par][:, bass.ds(star, 1)]).then_inc(sg("moe_star_sb"), 1)
                dve.wait_ge(sg("moe_star_sb"), e + 1)
                nc.vector.tensor_scalar(ov, code_b[par], 0.0, a_star[:, 0:1], ALU.min, ALU.mult)
                nc.vector.scalar_tensor_tensor(aa[par], code_b[par], 0.0, aa[par], ALU.max, ALU.mult).then_inc(sg("moe_act"), 1)
                dve.wait_ge(sg("moe_act"), 2 * e + 1)
                nc.vector.tensor_tensor(aa[par], aa[par], ov, ALU.subtract).then_inc(sg("moe_act"), 1)

            expert(0, 0, 0)
            expert(1, 1, 0)
            with dve.Fori(1, NE // 2) as i:
                expert(2 * i, 0, i)
                expert(2 * i + 1, 1, i)
            expert(NE - 1, 0, NE // 2)
            for k in range(KC):
                dve.wait_ge(sg("moe_down"), NE + k)
                nc.vector.tensor_tensor(chunk(ln_c, k), psum[:, (4 + 2 * k) * 512:(6 + 2 * k) * 512], chunk(h_t, k), ALU.add)\
                    .then_inc(sg("y"), 1)
                dve.wait_ge(sg("y"), 2 * KC + k + 1)
                residual_dve(dve, "y_out", 1, GB, ln_c, k)

        @block.gpsimd
        def _(pool):
            nc.gpsimd.memset(neg_half, -0.5).then_inc(sg("pool_set"), 1)
            nc.gpsimd.memset(small[0:1, 640:640 + NE].bitcast(I32), 0).then_inc(sg("pool_set"), 1)
            pool.wait_ge(sg("pool_set"), 1)
            rstd_pool(pool, "n0")
            for j in range(1, LUT):
                pool.wait_ge(sg("lut_tmp"), j + 1)
                if j > 1:
                    pool.wait_ge(sg("lut_pre"), j - 1)
                nc.gpsimd.tensor_tensor(lut_w[:, 0:LPRE], pre_tmp[:, 0:LPRE] if j == 1 else lut_w[:, 0:LPRE],
                                        pre_tmp[:, j * LPRE:j * LPRE + LPRE], ALU.add).then_inc(sg("lut_pre"), 1)
            pool.wait_ge(*norm("n0", "out"))
            for s in "qkv":
                nc.gpsimd.memset(by_batch(u[s])[:, :, 0:PAD], 0.0)
            i = nc.gpsimd.memset(rows_sb, 0.0)
            i.then_inc(sg("pool_set"), 1)
            pool.wait_ge(sg("a_sb"), 1)
            pool.wait_ge(sg("in_cst"), 16)

            def turn(h, hh, par, st):
                def blocks(t):
                    return by_tile(t[:, 0:T])

                def seams(t):
                    return t[:, T:BAND].rearrange("p (b j) -> p b j", j=PAD)

                def add(js):
                    for j in js:
                        if j == 0 and par == 0:
                            continue
                        pool.wait_ge(sg("a0_lut_tmp"), LTURN * h + j + 1)
                        if j == 1 and par == 0:
                            if since(h, 1):
                                pool.wait_ge(sg("a0_lut_out"), 16 * hh)
                            nc.gpsimd.tensor_tensor(lacc, lt[0], lt[1], ALU.add).then_inc(sg("a0_lut_add"), 2)
                        else:
                            pool.wait_ge(sg("a0_lut_add"), LTURN * h + j)
                            nc.gpsimd.tensor_tensor(lacc, lacc, lt[j], ALU.add).then_inc(sg("a0_lut_add"), 1)

                if 1 in st:
                    nc.gpsimd.tensor_copy(a_head, a_tok[:, bass.ds(h * NT, NT)]).then_inc(sg("a0_a"), 1)
                    pool.wait_ge(sg("a0_a"), h + 1)
                    pool.wait_ge(sg("a0_b"), 16 * (h + 1))
                    nc.gpsimd.tensor_tensor(seams(gate), by_batch(gate[:, 0:T])[:, :, P:P + PAD],
                                            over_cols(a_head.rearrange("p (b j) -> p b j", j=2)[:, :, 0], PAD),
                                            ALU.mult).then_inc(sg("a0_ab_seam"), 1)
                    pool.wait_ge(sg("a0_ab_seam"), h + 1)
                    nc.gpsimd.tensor_tensor(blocks(gate), blocks(gate), over_cols(a_head, P), ALU.mult).then_inc(sg("a0_ab"), 1)
                if 2 in st:
                    pool.wait_ge(sg("a0_ssq_s"), h)
                    if since(h, 2):
                        pool.wait_ge(sg("a0_g"), h - 1)
                        pool.wait_ge(sg("a0_sqo"), h - 1)
                    nc.gpsimd.tensor_tensor(rqk[1 - par], ssq_s, neg_half, ALU.pow).then_inc(sg("a0_rqk"), 1)
                if 1 in st:
                    for j, s in enumerate("qk"):
                        pool.wait_ge(sg("a0_conv_" + s), 3 * h + 3)
                        if since(h, 1):
                            pool.wait_ge(sg("a0_S"), h)
                        nc.gpsimd.tensor_tensor(by_batch(rot[s]), by_batch(c_[s]), over_tiles(cos_t, B), ALU.mult)\
                            .then_inc(sg("a0_rc_" + s), 1)
                        pool.wait_ge(sg("a0_sw_" + s), 32 * (h + 1))
                        nc.gpsimd.tensor_tensor(by_batch(sw[s]), by_batch(sw[s]), over_tiles(sin_t, B), ALU.mult)\
                            .then_inc(sg("a0_rs_" + s), 1)
                        add(range(j * LTURN // 2, (j + 1) * LTURN // 2))

            turns0(pool, turn)
            rstd_pool(pool, "r0")
            for j in range(1, LUT):
                pool.wait_ge(sg("lut_tmp"), LUT + j + 1)
                post_sum(pool, nc.gpsimd, j, "lut_post_pool", slice(LPOST // 2, LPOST))
            rstd_pool(pool, "n1")
            def weights(h, par):
                pool.wait_ge(sg("a1_code"), 80 * (h + 1))
                if since(h, 2):
                    pool.wait_ge(sg("a1_v"), h - 1)
                nc.gpsimd.tensor_tensor(w1[par], code, scl, ALU.mult).then_inc(sg("a1_wmul"), 1)

            def weights_lower(h, par):
                pool.wait_ge(sg("a1_w_hi"), h + 1)
                nc.gpsimd.tensor_tensor(w1_l[par], w1[par][:, 0:QK], w1_h[par].bitcast(F32), ALU.subtract)\
                    .then_inc(sg("a1_w_lo"), 1)

            weights(0, 0)
            pool.wait_ge(sg("in_wo"), 80)
            nc.gpsimd.tensor_tensor(wo_c, wo_c, wo_s, ALU.mult).then_inc(sg("a1_womul"), 1)
            rstd_pool(pool, "n2")
            weights_lower(0, 0)
            weights(1, 1)
            weights_lower(1, 1)
            with pool.Fori(1, H // 2) as i:
                for par in range(2):
                    weights(2 * i + par, par)
                    weights_lower(2 * i + par, par)
            rstd_pool(pool, "n3")
            pool.wait_ge(*norm("n3", "out"))
            nc.gpsimd.memset(code_t[E:NE, :], 1.0).then_inc(sg("pool_set"), 1)
            pool.wait_ge(sg("pool_set"), 4)
            rstd_pool(pool, "n4")

            def lower_13(e, par):
                pool.wait_ge(sg("moe_w13_hi"), e + 1)
                if since(e, 2):
                    pool.wait_ge(sg("moe_u"), e - 1)
                nc.gpsimd.tensor_tensor(el[par][:, 0:2 * D], we[par][:, 0:2 * D], eh[par][:, 0:2 * D].bitcast(F32), ALU.subtract)\
                    .then_inc(sg("moe_w13_lo"), 1)

            def lower(e, par, ahead=True):
                pool.wait_ge(sg("moe_w2_hi"), e + 1)
                if since(e, 2):
                    pool.wait_ge(sg("moe_down"), e - 1)
                nc.gpsimd.tensor_tensor(el[par][:, 2 * D:EW], we[par][:, 2 * D:EW], eh[par][:, 2 * D:EW].bitcast(F32),
                                        ALU.subtract).then_inc(sg("moe_w2_lo"), 1)
                pool.wait_ge(sg("moe_hi"), e + 1)
                nc.gpsimd.tensor_tensor(aa_l[par], aa[par], aa_h[par].bitcast(F32), ALU.subtract).then_inc(sg("moe_lo"), 1)
                if ahead:
                    lower_13(e + 2, par)

            lower_13(0, 0)
            lower_13(1, 1)
            pool.wait_ge(sg("in_hi"), KC + 1)
            nc.gpsimd.tensor_tensor(xr_l, xr, xr_h.bitcast(F32), ALU.subtract).then_inc(sg("in_lo"), 1)
            lower(0, 0)
            lower(1, 1)
            with pool.Fori(1, NE // 2 - 1) as i:
                lower(2 * i, 0)
                lower(2 * i + 1, 1)
            lower(NE - 3, 0)
            lower(NE - 2, 1, ahead=False)
            lower(NE - 1, 0, ahead=False)

def kernel(**inputs):
    import numpy as np
    import concourse.bacc as _bacc
    from concourse.bass_utils import run_bass_kernel_spmd as _run

    x = {k: np.asarray(v) for k, v in inputs.items()}

    def rows(w):
        return np.ascontiguousarray(w.reshape(-1, P, w.shape[1]).transpose(1, 0, 2)).reshape(P, -1)

    def heads(ws):
        return np.ascontiguousarray(np.stack([w.reshape(KC, P, H, HD) for w in ws]).transpose(3, 2, 0, 1, 4)).reshape(H, P, -1)

    def per_head(v):
        return v.reshape(H, P).T

    f = np.float32
    d_, s_ = np.arange(P), np.arange(S)
    inv = (1.0 / f(1000000.0) ** (np.arange(0, HD, 2, dtype=f) / f(HD))).astype(f)
    ang = (s_.astype(f)[None, :] * inv[:, None]).astype(f)
    lag = d_[None, :] - d_[:, None]
    seam_lag = P + np.arange(PAD)[None, :] - d_[:, None]
    cst = np.concatenate([
        np.eye(P), np.ones((P, P)), np.full((P, P), 1.0 / D), lag > 0,
        ((lag >= 0) & (lag < TAPS)) * (0.5 * SCALE), (seam_lag < TAPS) * (0.5 * SCALE),
        np.cos(np.concatenate([ang, ang])), np.concatenate([-np.sin(ang), np.sin(ang)]),
        np.tile(np.arange(E), (P, 1)), d_[:, None] + P * np.arange(NT)[None, :],
        np.tile(np.arange(4 * NT - 1) == 2 * NT - 1, (P, 1))], axis=1).astype(f)
    idx = np.zeros((P, LUTC), np.int32)
    idx[:, 0:UPC] = rows(x["L0_ffn_gate_idx"].T)
    idx[:, UPC:2 * UPC] = rows(x["L0_ffn_up_idx"].T)
    down = np.zeros((MT * P, D), np.int32)
    down[0:INTER] = x["L0_ffn_down_idx"].T
    idx[:, 2 * UPC:] = rows(down)
    qkv_scales = np.stack([x[f"L1_attn_w{j}_scales"].reshape(KC, 4, H, HD) for j in "qkv"])
    moe = np.zeros((NE, P, EW), f)
    moe[0:E, :, 0:2 * D] = x["L1_ffn_w13"].reshape(E, KC, P, D).transpose(0, 2, 1, 3).reshape(E, P, 2 * D)
    moe[0:E, :, 2 * D:] = x["L1_ffn_w2"]
    moe[E, :, 0:2 * D] = rows(np.concatenate([x["L1_ffn_shared_gate_w"], x["L1_ffn_shared_up_w"]], axis=1))
    moe[E, :, 2 * D:] = x["L1_ffn_shared_down_w"]
    arrays = {
        "x": rows(x["L0_attn_x"].reshape(T, D).T),
        "c0": rows(x["L0_c"].T), "c1": rows(x["L1_c"].T),
        "wmod0": rows(x["L0_wmod"]), "wmod1": rows(x["L1_wmod"]),
        "cst": cst,
        "par_in": np.concatenate(
            [x[f"L0_attn_conv_{j}_w"].reshape(H, P, TAPS).transpose(1, 0, 2).reshape(P, -1) for j in "qkv"]
            + [per_head(x["L0_attn_norm_w"]), rows(np.concatenate([x["L0_attn_Wb"], x["L0_attn_Wa"]], axis=1))]
            + [per_head(x[f"L1_attn_b{j}"]) for j in "qkv"]
            + [x["L1_attn_bo"].reshape(KC, P).T, x["L1_ffn_norm_w"].reshape(KC, P).T, rows(x["L1_ffn_gate_w"].T)], axis=1),
        "lut": x["L0_ffn_lut"].reshape(1, LUT),
        "idx_pre": idx[:, 0:LPRE], "idx_post": idx[:, LUTC - LPOST:],
        "idx": idx[:, LPRE:LUTC - LPOST].reshape(P, H // 2, LW).transpose(1, 0, 2),
        "w_qkvz": heads([x[f"L0_attn_W{j}"] for j in "qkvz"]),
        "w_out": rows(x["L0_attn_Wout"]),
        "qkv_codes": heads([x[f"L1_attn_w{j}_codes"] for j in "qkv"]),
        "qkv_scales": np.ascontiguousarray(qkv_scales.transpose(3, 2, 0, 1, 4)).reshape(H, 4, QKV),
        "wo_codes": rows(x["L1_attn_wo_codes"]),
        "wo_scales": np.ascontiguousarray(x["L1_attn_wo_scales"].reshape(H, 4, D).transpose(1, 0, 2)).reshape(4, H * D),
        "w_moe": moe,
    }
    nc = _bacc.Bacc("TRN2", target_bir_lowering=False, num_devices=1)
    arrays = {k: np.ascontiguousarray(v) for k, v in arrays.items()}
    aps = {k: nc.dram_tensor("in_" + k, v.shape, mybir.dt.from_np(v.dtype), kind="ExternalInput").ap() for k, v in arrays.items()}
    out = nc.dram_tensor("out_0", (P, KC * T), F32, kind="ExternalOutput").ap()
    b_rows = nc.dram_tensor("b_rows", (H, T), F32, kind="Internal").ap()
    code_rows = nc.dram_tensor("code_rows", (NE, T), F32, kind="Internal").ap()
    build(nc, aps, out, b_rows, code_rows)
    r = _run(nc, [{"in_" + k: v for k, v in arrays.items()}], core_ids=[0])
    y = r.results[0]["out_0"]
    return np.ascontiguousarray(y.reshape(P, KC, B, S).transpose(2, 3, 1, 0)).reshape(B, S, D)
```
